# Optimizing a Trainium2 kernel written in Bass

```python
import numpy as np
import jax
import jax.numpy as jnp

def _softmax(x, axis=-1):
    return jax.nn.softmax(x, axis=axis)

def _gelu(x):
    return jax.nn.gelu(x, approximate=True)

def _silu(x):
    return jax.nn.silu(x)

def _sigmoid(x):
    return jax.nn.sigmoid(x)

def _layernorm(x, axis=-1, eps=1e-05):
    m = jnp.mean(x, axis=axis, keepdims=True)
    v = jnp.var(x, axis=axis, keepdims=True)
    return (x - m) / jnp.sqrt(v + eps)

def _scatter_add(tgt, idx, src, axis=0):
    return tgt.at[idx].add(src)

def _segment_sum(src, seg, n):
    return jax.ops.segment_sum(src, seg, n)
kernel_name = 'mk_decoder_postln_d1_seqx_r8_1de5f0'

def setup_inputs(seed: int=0):
    np.random.seed(seed)
    _w = jnp.asarray

    def _rec_inputs():
        import jax
        import jax.numpy as jnp
        _rk = jax.random.key(seed)
        x = -0.0002928 + 1 * jax.random.normal(jax.random.fold_in(_rk, 1), (4, 512, 128), jnp.float32)
        _lenS = 512 - jax.random.randint(jax.random.fold_in(_rk, 7), (4,), 0, max(1, 512 // 4) + 1, jnp.int32)
        _lenS2 = 77 - jax.random.randint(jax.random.fold_in(_rk, 8), (4,), 0, max(1, 77 // 4) + 1, jnp.int32)
        _ctx_1024P = jax.random.normal(jax.random.fold_in(_rk, 11), (4, 16, 128), jnp.float32)
        _ctx_1024c = jax.random.dirichlet(jax.random.fold_in(_rk, 511), 0.3 * jnp.ones((16,), jnp.float32), (4, 77))
        _ctx_1024t = jnp.einsum('bsk,bkd->bsd', _ctx_1024c, _ctx_1024P)
        _ctx_1024t = _ctx_1024t * jax.lax.rsqrt(jnp.mean(jnp.square(_ctx_1024t)) + 1e-12) * 0.953939
        ctx_1024 = -1.39393e-06 + 0.999914 * (_ctx_1024t + 0.3 * jax.random.normal(jax.random.fold_in(_rk, 611), (4, 77, 128), jnp.float32))
        return (x, ctx_1024)
    x, ctx_1024 = _rec_inputs()

    def _L0_attn_setup():
        import jax, jax.numpy as jnp
        import numpy as np
        NUM_HEADS = 16
        EMB = 128
        DH = 64
        B, S = (4, 256)
        key = jax.random.key(seed)
        ks = jax.random.split(key, 9)
        sc = lambda fan_in: 1.0 / np.sqrt(fan_in)
        Wq = jax.random.uniform(ks[0], (NUM_HEADS, EMB, DH), minval=-sc(EMB), maxval=sc(EMB))
        Wk = jax.random.uniform(ks[1], (NUM_HEADS, EMB, DH), minval=-sc(EMB), maxval=sc(EMB))
        Wv = jax.random.uniform(ks[2], (NUM_HEADS, EMB, DH), minval=-sc(EMB), maxval=sc(EMB))
        bq = jax.random.uniform(ks[3], (NUM_HEADS, DH), minval=-sc(EMB), maxval=sc(EMB))
        bk = jax.random.uniform(ks[4], (NUM_HEADS, DH), minval=-sc(EMB), maxval=sc(EMB))
        bv = jax.random.uniform(ks[5], (NUM_HEADS, DH), minval=-sc(EMB), maxval=sc(EMB))
        Wo = jax.random.uniform(ks[6], (NUM_HEADS * DH, EMB), minval=-sc(NUM_HEADS * DH), maxval=sc(NUM_HEADS * DH))
        bo = jax.random.uniform(ks[7], (EMB,), minval=-sc(NUM_HEADS * DH), maxval=sc(NUM_HEADS * DH))
        x = jax.random.normal(ks[8], (B, S, EMB), dtype=jnp.float32)
        return {'x': x, 'Wq': Wq, 'Wk': Wk, 'Wv': Wv, 'bq': bq, 'bk': bk, 'bv': bv, 'Wo': Wo, 'bo': bo}
    _L0_attn_all = _L0_attn_setup()
    _L0_attn_in = {k: v for k, v in _L0_attn_all.items() if k in ('Wq', 'Wk', 'Wv', 'bq', 'bk', 'bv', 'Wo', 'bo')}
    del _L0_attn_all

    def _L0_xattn_setup():
        import jax, jax.numpy as jnp
        import numpy as np
        EMBED_DIM = 128
        NUM_HEADS = 16
        DIM_K = EMBED_DIM // NUM_HEADS
        B, S = (2, 256)
        key = jax.random.key(seed)
        ks = jax.random.split(key, 7)
        scale = 1.0 / np.sqrt(EMBED_DIM)
        return {'query': jax.random.normal(ks[0], (B, S, EMBED_DIM), dtype=jnp.float32), 'key': jax.random.normal(ks[1], (B, S, EMBED_DIM), dtype=jnp.float32), 'value': jax.random.normal(ks[2], (B, S, EMBED_DIM), dtype=jnp.float32), 'Wq': jax.random.normal(ks[3], (EMBED_DIM, EMBED_DIM), dtype=jnp.float32) * scale, 'Wk': jax.random.normal(ks[4], (EMBED_DIM, EMBED_DIM), dtype=jnp.float32) * scale, 'Wv': jax.random.normal(ks[5], (EMBED_DIM, EMBED_DIM), dtype=jnp.float32) * scale, 'Wo': jax.random.normal(ks[6], (EMBED_DIM, EMBED_DIM), dtype=jnp.float32) * scale}
    _L0_xattn_all = _L0_xattn_setup()
    _L0_xattn_in = {k: v for k, v in _L0_xattn_all.items() if k in ('Wq', 'Wk', 'Wv', 'Wo')}
    del _L0_xattn_all

    def _L0_ffn_setup():
        import jax, jax.numpy as jnp
        import numpy as np
        FEATURES = 128
        D_IN = 128

        def fp8_gemm_optimized(x, input_scale, kernel, kernel_scale):
            s_in = input_scale[0]
            s_k = kernel_scale[0]
            x_q = (x.astype(jnp.float32) / s_in).astype(jnp.float8_e4m3fn)
            k_q = (kernel.astype(jnp.float32) / s_k).astype(jnp.float8_e4m3fn)
            y = jnp.dot(x_q.astype(jnp.float32), k_q.astype(jnp.float32), preferred_element_type=jnp.float32)
            return y * (s_in * s_k)
        key = jax.random.key(seed)
        kx, kk, kb = jax.random.split(key, 3)
        x = jax.random.normal(kx, (4, 1024, D_IN), dtype=jnp.float32)
        limit = np.sqrt(6.0 / (D_IN + FEATURES)).astype(np.float32)
        kernel = jax.random.uniform(kk, (D_IN, FEATURES), dtype=jnp.float32, minval=-limit, maxval=limit).astype(jnp.bfloat16)
        input_scale = jnp.ones((1,), dtype=jnp.float32)
        kernel_scale = jnp.ones((1,), dtype=jnp.float32)
        bias = jnp.zeros((FEATURES,), dtype=jnp.bfloat16)
        return {'x': x, 'kernel': kernel, 'input_scale': input_scale, 'kernel_scale': kernel_scale, 'bias': bias}
    _L0_ffn_all = _L0_ffn_setup()
    _L0_ffn_in = {k: v for k, v in _L0_ffn_all.items() if k in ('kernel', 'input_scale', 'kernel_scale', 'bias')}
    del _L0_ffn_all
    return {'x': x, 'ctx_1024': ctx_1024, 'L0_attn_Wq': _L0_attn_in['Wq'], 'L0_attn_Wk': _L0_attn_in['Wk'], 'L0_attn_Wv': _L0_attn_in['Wv'], 'L0_attn_bq': _L0_attn_in['bq'], 'L0_attn_bk': _L0_attn_in['bk'], 'L0_attn_bv': _L0_attn_in['bv'], 'L0_attn_Wo': _L0_attn_in['Wo'], 'L0_attn_bo': _L0_attn_in['bo'], 'L0_xattn_Wq': _L0_xattn_in['Wq'], 'L0_xattn_Wk': _L0_xattn_in['Wk'], 'L0_xattn_Wv': _L0_xattn_in['Wv'], 'L0_xattn_Wo': _L0_xattn_in['Wo'], 'L0_ffn_kernel': _L0_ffn_in['kernel'], 'L0_ffn_input_scale': _L0_ffn_in['input_scale'], 'L0_ffn_kernel_scale': _L0_ffn_in['kernel_scale'], 'L0_ffn_bias': _L0_ffn_in['bias']}

def reference(x, ctx_1024, L0_attn_Wq, L0_attn_Wk, L0_attn_Wv, L0_attn_bq, L0_attn_bk, L0_attn_bv, L0_attn_Wo, L0_attn_bo, L0_xattn_Wq, L0_xattn_Wk, L0_xattn_Wv, L0_xattn_Wo, L0_ffn_kernel, L0_ffn_input_scale, L0_ffn_kernel_scale, L0_ffn_bias):
    import jax
    import jax.numpy as jnp

    def _L0_attn_ref(x, Wq, Wk, Wv, bq, bk, bv, Wo, bo):
        import jax, jax.numpy as jnp
        import numpy as np
        NUM_HEADS = 16
        EMB = 128
        DH = 64
        B, S = (4, 256)
        seq_len = x.shape[1]
        q = jnp.einsum('bse,hed->bhsd', x, Wq) + bq[None, :, None, :]
        k = jnp.einsum('bse,hed->bhsd', x, Wk) + bk[None, :, None, :]
        v = jnp.einsum('bse,hed->bhsd', x, Wv) + bv[None, :, None, :]
        scores = jnp.einsum('bhsd,bhtd->bhst', q, k) / jnp.sqrt(jnp.float32(DH))
        causal = jnp.tril(jnp.ones((seq_len, seq_len), dtype=bool))
        scores = jnp.where(causal[None, None, :, :], scores, -jnp.inf)
        attn = jax.nn.softmax(scores, axis=-1)
        out = jnp.einsum('bhst,bhtd->bhsd', attn, v)
        out = out.transpose(0, 2, 1, 3).reshape(x.shape[0], seq_len, NUM_HEADS * DH)
        return out @ Wo + bo

    def _L0_xattn_ref(query, key, value, Wq, Wk, Wv, Wo):
        import jax, jax.numpy as jnp
        import numpy as np
        EMBED_DIM = 128
        NUM_HEADS = 16
        DIM_K = EMBED_DIM // NUM_HEADS
        B, S = (2, 256)
        b, s, e = query.shape

        def proj(x, W):
            y = x @ W.T
            return y.reshape(b, -1, NUM_HEADS, DIM_K).transpose(0, 2, 1, 3)
        q = proj(query, Wq)
        k = proj(key, Wk)
        v = proj(value, Wv)
        scores = jnp.einsum('bhqd,bhkd->bhqk', q, k) / jnp.sqrt(jnp.float32(DIM_K))
        attn = jax.nn.softmax(scores, axis=-1)
        x = jnp.einsum('bhqk,bhkd->bhqd', attn, v)
        x = x.transpose(0, 2, 1, 3).reshape(b, -1, e)
        return x @ Wo.T

    def _L0_ffn_ref(x, kernel, input_scale, kernel_scale, bias):
        import jax, jax.numpy as jnp
        import numpy as np
        FEATURES = 128
        D_IN = 128

        def fp8_gemm_optimized(x, input_scale, kernel, kernel_scale):
            s_in = input_scale[0]
            s_k = kernel_scale[0]
            x_q = (x.astype(jnp.float32) / s_in).astype(jnp.float8_e4m3fn)
            k_q = (kernel.astype(jnp.float32) / s_k).astype(jnp.float8_e4m3fn)
            y = jnp.dot(x_q.astype(jnp.float32), k_q.astype(jnp.float32), preferred_element_type=jnp.float32)
            return y * (s_in * s_k)
        dtype = jnp.bfloat16
        x = x.astype(dtype)
        orig_shape = x.shape
        x2 = x.reshape(-1, x.shape[-1])
        y = fp8_gemm_optimized(x2, input_scale, kernel, kernel_scale)
        y = y.astype(dtype) + bias
        return y.reshape(orig_shape[:-1] + (FEATURES,))
    x = _layernorm(x + _L0_attn_ref(x, L0_attn_Wq, L0_attn_Wk, L0_attn_Wv, L0_attn_bq, L0_attn_bk, L0_attn_bv, L0_attn_Wo, L0_attn_bo), axis=-1)
    x = _layernorm(x + _L0_xattn_ref(x, ctx_1024, ctx_1024, L0_xattn_Wq, L0_xattn_Wk, L0_xattn_Wv, L0_xattn_Wo), axis=-1)
    x = _layernorm(x + _L0_ffn_ref(x, L0_ffn_kernel, L0_ffn_input_scale, L0_ffn_kernel_scale, L0_ffn_bias), axis=-1)
    return x

_drawn_inputs = setup_inputs


def setup_inputs(seed=0):
    import zlib

    import numpy as np

    out = dict(_drawn_inputs(seed))
    spreads = {'L0_ffn_bias': (0.0, 0.1)}
    factors = {'L0_attn_Wq': 2.947, 'L0_attn_Wk': 2.939, 'L0_attn_bq': 8.0, 'L0_attn_bk': 8.0}
    for name, (base, spread) in spreads.items():
        noise = np.random.default_rng([zlib.crc32(name.encode()), seed]).standard_normal(out[name].shape)
        drawn = base * np.exp(spread * noise) if base else spread * noise
        out[name] = jnp.asarray(drawn.astype(out[name].dtype))
    for name, factor in factors.items():
        out[name] = (out[name] * factor).astype(out[name].dtype)
    return out
```

```python
import numpy as np
import concourse.bass as bass
from concourse import mybir
from contextlib import ExitStack

B, S, E = 4, 512, 128
H, D = 16, 64
T = 128
NT = S // T
PAIRS = H // 2
UNITS = PAIRS * B


def self_attention(nc, banks, attn_t, xT, w_qkv, b_qk, b_v, causal, ident):
    f32, f32r, bf16 = mybir.dt.float32, mybir.dt.float32r, mybir.dt.bfloat16
    ALU, ACT = mybir.AluOpType, mybir.ActivationFunctionType
    ctx = ExitStack()
    with ctx:
        sb = lambda name, shape, dt=f32: ctx.enter_context(nc.sbuf_tensor(name, shape, dt))
        sem = lambda name: ctx.enter_context(nc.semaphore(name))

        x_t = sb("x_t", [128, B * S])
        x_hi = sb("x_hi", [128, B * S], f32r)
        x_lo = sb("x_lo", [128, B * S], f32r)
        w_pair = sb("w_pair", [128, 3, 2 * D])
        w_hi = sb("w_hi", [128, 2, 2 * D], f32r)
        w_lo = sb("w_lo", [128, 2, 2 * D], f32r)
        bias_qk = sb("bias_qk", [128, 2, PAIRS])
        bias_pair = sb("bias_pair", [128, 2, 2])
        bias_v = sb("bias_v", [128, PAIRS, 2 * D])
        bias_v_pair = sb("bias_v_pair", [128, 2 * D])
        neg_mask = sb("neg_mask", [128, S])
        ident_b = sb("ident_b", [128, 128], bf16)
        ones64 = sb("ones64", [128, D])
        q_hihi = sb("q_hihi", [128, 2, 2, S], f32r)
        q_lo = sb("q_lo", [128, 2, 2, S], f32r)
        k_hilo = sb("k_hilo", [128, 2, 2, S], f32r)
        k_hi1 = sb("k_hi1", [128, 2, 2, S], f32r)
        v_nat = sb("v_nat", [128, 4, NT, 2 * D])
        row_max = sb("row_max", [128, 2, NT])
        shift = sb("shift", [128, 2, NT, 2], bf16)
        junk = sb("junk", [128, NT, S], bf16)
        probs = sb("probs", [128, 2, 2, 3 * S])
        r_sum = sb("r_sum", [128, S])

        aux = [banks[:, 0, :], banks[:, 1, :]]
        sm = [banks[:, 2, :], banks[:, 3, :]]
        st = banks[:, 4:7, :].rearrange("p b c -> p (b c)")
        o_ps = banks[:, 7, :]

        x_in, const_in, w_in = sem("x_in"), sem("const_in"), sem("w_in")
        x_split, w_split, zeroed = sem("x_split"), sem("w_split"), sem("zeroed")
        q_done, k_done, v_done, mrow_done = sem("q_done"), sem("k_done"), sem("v_done"), sem("mrow_done")
        sm_done, st_done, o_done, r_done = sem("sm_done"), sem("st_done"), sem("o_done"), sem("r_done")
        qh_out, kh_out, s_out, exp_out = sem("qh_out"), sem("kh_out"), sem("s_out"), sem("exp_out")
        ql_out, kl_out, v_out = sem("ql_out"), sem("kl_out"), sem("v_out")
        max_out, sh_hi, sh_out, rr_out, o_out = sem("max_out"), sem("sh_hi"), sem("sh_out"), sem("rr_out"), sem("o_out")
        q_dup, k_dup = [[sem(f"{n}_dup{i}") for i in range(2)] for n in "qk"]
        masked = sem("masked")
        w_hi_out, passed = sem("w_hi_out"), sem("passed")
        bias_out = sem("bias_out")

        CONSTS = 16 * 4
        KEYS = {0: (0, 0), 1: (512, 128), 3: (1024, 256), 2: (1280, 256)}
        SPLIT = [slice(0, D), slice(D, 2 * D)]
        OTHER = [slice(D, 2 * D), slice(0, D)]

        def least(n):
            return max(n, 0) if isinstance(n, int) else n

        def has(n, d):
            return n is None or 0 <= n + d < UNITS

        block = ctx.enter_context(nc.Block())

        @block.tensor
        def _(pe):
            mm = nc.tensor.matmul

            def sm_piece(v, par, h, k):
                pe.wait_ge(max_out, least(v * 6 + (3 * h + k - 1)))
                dst = sm[(3 * h + k) % 2]
                for i, at, n in (((3, 0, 512),), ((2, 0, 384),), ((1, 0, 256), (0, 256, 256)))[k]:
                    last = mm(dst[:, at:at + n], q_hihi[:, par, h, i * T:(i + 1) * T],
                              k_hilo[:, par, h, 0:n], start=True, stop=True)
                last.then_inc(sm_done, 1)

            def scores(u, par, h):
                def both(j, n):
                    at, q0 = KEYS[j]
                    mm(st[:, at:at + n], k_hilo[:, par, h, j * T:(j + 1) * T],
                       q_hihi[:, par, h, q0:S], start=True, stop=False)
                    return mm(st[:, at:at + n], k_hi1[:, par, h, j * T:(j + 1) * T],
                              q_lo[:, par, h, q0:S], start=False, stop=True)
                pe.wait_ge(exp_out, least(u * 4 + (2 * h - 1)))
                pe.wait_ge(s_out, least(u * 2 + (1 + h)))
                both(0, 512)
                both(1, 384).then_inc(st_done, 1)
                pe.wait_ge(exp_out, least(u * 4 + 2 * h))
                both(3, 256)
                both(2, 256).then_inc(st_done, 1)

            def weighted(dst, u, par, m, js, stationary):
                for j in js:
                    at, q0 = KEYS[j]
                    if j == 3:
                        at, q0 = at + T, q0 + T
                    for h in (0, 1):
                        last = mm(dst[SPLIT[h], q0:S], stationary(j, h), probs[:, par, h, at:at + S - q0],
                                  start=(j == 0), stop=(j == NT - 1))
                return last

            def slot(u, m, n, at):
                par, nxt = m % 2, (m + 1) % 2
                me, prev, v = has(n, 0), has(n, -1), has(n, 2)
                nx = has(n, 1)
                if me:
                    pe.wait_ge(k_dup[par], least((at(0, 2) + 1) * 32))
                    scores(u, par, 0)
                if nx:
                    pe.wait_ge(q_dup[nxt], least((at(1, 2) + 1) * 32))
                    pe.wait_ge(kl_out, least((u + 2) * 2))
                    pe.wait_ge(kh_out, least((u + 2) * 2))
                    sm_piece(u + 1, nxt, 0, 0)
                if prev:
                    pe.wait_ge(masked, least(u * 2))
                    if not nx:
                        pe.wait_ge(o_out, least(u - 1))
                    vs = lambda j, h: v_nat[:, (m - 1) % 4, j, SPLIT[h]]
                    weighted(o_ps, u - 1, nxt, m, (0, 1), vs)
                if nx:
                    sm_piece(u + 1, nxt, 0, 1)
                    sm_piece(u + 1, nxt, 0, 2)
                if prev:
                    weighted(o_ps, u - 1, nxt, m, (2, 3), vs).then_inc(o_done, 1)
                if me:
                    scores(u, par, 1)
                if prev:
                    pe.wait_ge(v_out, least(min(u + 2, UNITS) if isinstance(u, int) else u + 2))
                    weighted(aux[0], u - 1, nxt, m, (0, 1, 2, 3), lambda j, h: ones64[:, :]).then_inc(r_done, 1)
                if v:
                    b = (m + 2) % 4
                    if b == 0:
                        pe.wait_ge(w_split, least(at(2, 4) + 1))
                    xs = slice(b * S, (b + 1) * S)
                    pe.wait_ge(rr_out, least(u))
                    for w, (dst, done) in enumerate(((aux[0], q_done), (aux[1], k_done))):
                        if w == 1:
                            pe.wait_ge(s_out, least((u + 1) * 2))
                        mm(dst[:, :], w_hi[:, w, :], x_hi[:, xs], start=True, stop=False)
                        mm(dst[:, :], w_hi[:, w, :], x_lo[:, xs], start=False, stop=False)
                        mm(dst[:, :], w_lo[:, w, :], x_hi[:, xs], start=False, stop=True).then_inc(done, 1)
                if nx:
                    for k in range(3):
                        sm_piece(u + 1, nxt, 1, k)
                if v:
                    pe.wait_ge(qh_out, least((u + 3) * 2))
                    pe.wait_ge(ql_out, least((u + 3) * 2))
                    for i in range(NT):
                        last = mm(aux[0][:, i * T:(i + 1) * T], x_t[:, b * S + i * T:b * S + (i + 1) * T],
                                  w_pair[:, 2, :], start=True, stop=True)
                    last.then_inc(v_done, 1)
                if nx:
                    pe.wait_ge(sh_out, least(u + 2))
                    pe.wait_ge(kh_out, least((u + 3) * 2 if v else 2 * UNITS))
                    pe.wait_ge(kl_out, least((u + 3) * 2 if v else 2 * UNITS))
                    for h in (0, 1):
                        rows = slice(64, 66) if h == 0 else slice(0, 2)
                        for i in range(NT):
                            last = mm(aux[1][rows, i * T:(i + 1) * T], shift[:, h, i, :], ident_b[:, :],
                                      start=True, stop=True)
                    last.then_inc(mrow_done, 1)

            pe.wait_ge(x_split, 2)
            pe.wait_ge(const_in, CONSTS)
            pe.wait_ge(zeroed, 1)

            for u in (-2, -1, 0):
                slot(u, u % 4, u, lambda d, c: (u + d) // c)
            with pe.Fori(0, (UNITS - 4) // 4) as p:
                for k in range(1, 5):
                    slot(p * 4 + k, k % 4, None, lambda d, c: p * (4 // c) + (k + d) // c)
            for u in range(UNITS - 3, UNITS + 1):
                slot(u, u % 4, u, lambda d, c: (u + d) // c)

        @block.scalar
        def _(act):
            def slot(u, m, n, at):
                par, nxt = m % 2, (m + 1) % 2
                if has(n, 0):
                    for h in (0, 1):
                        act.wait_ge(st_done, least(u * 4 + (2 * h + 1)))
                        nc.scalar.activation(probs[:, par, h, 0:896], st[:, 0:896], ACT.Exp,
                                             scale=D ** -0.5).then_inc(exp_out, 1)
                        act.wait_ge(st_done, least(u * 4 + (2 * h + 2)))
                        nc.scalar.activation(probs[:, par, h, 1152:1536], st[:, 1152:1536], ACT.Exp,
                                             scale=D ** -0.5).then_inc(exp_out, 1)
                if has(n, 2):
                    if (m + 2) % 4 == 0:
                        act.wait_ge(w_split, least(at(2, 4) + 1))
                    for w, (src, done, dst, out) in enumerate(((aux[0], q_done, q_hihi, qh_out),
                                                               (aux[1], k_done, k_hilo, kh_out))):
                        act.wait_ge(done, least(u + 3))
                        for h in (0, 1):
                            nc.scalar.activation(dst[SPLIT[h], par, h, :], src[SPLIT[h], :], ACT.Identity,
                                                 bias=bias_pair[SPLIT[h], 0, w:w + 1]).then_inc(out, 1)
                if has(n, 1):
                    act.wait_ge(mrow_done, least(u + 2))
                    nc.scalar.copy(q_lo[64:66, nxt, 0, :], aux[1][64:66, :]).then_inc(s_out, 1)
                    nc.scalar.copy(q_lo[0:2, nxt, 1, :], aux[1][0:2, :]).then_inc(s_out, 1)

            act.wait_ge(x_in, 16)
            nc.scalar.copy(x_hi[:, :], x_t[:, :]).then_inc(x_split, 1)
            for u in (-2, -1, 0):
                slot(u, u % 4, u, lambda d, c: (u + d) // c)
            with act.Fori(0, (UNITS - 4) // 4) as p:
                for k in range(1, 5):
                    slot(p * 4 + k, k % 4, None, lambda d, c: p * (4 // c) + (k + d) // c)
            for u in range(UNITS - 3, UNITS + 1):
                slot(u, u % 4, u, lambda d, c: (u + d) // c)

        @block.vector
        def _(dve):
            def maxima(v, h):
                dve.wait_ge(sh_out, least(v))
                dve.wait_ge(max_out, least(v * 6 + 3 * h))
                for k, pieces in enumerate((((3, 0),), ((2, 0),), ((1, 0), (0, 256)))):
                    dve.wait_ge(sm_done, least(v * 6 + (3 * h + k + 1)))
                    dve.sem_inc(passed, 1)
                    for i, at in pieces:
                        n = (i + 1) * T
                        last = nc.vector.tensor_tensor_reduce(
                            out=junk[:, i, 0:n], in0=sm[(3 * h + k) % 2][:, at:at + n],
                            in1=neg_mask[:, S - n:S], scale=1.0, scalar=-3.0e38,
                            op0=ALU.add, op1=ALU.max, accum_out=row_max[:, h, i:i + 1])
                    last.then_inc(max_out, 1)

            def slot(u, m, n, at):
                par, nxt = m % 2, (m + 1) % 2
                if has(n, 1):
                    maxima(u + 1, 0)
                if has(n, -1):
                    b = (m - 1) % 4
                    dve.wait_ge(r_done, least(u))
                    nc.vector.reciprocal(r_sum[:, :], aux[0][:, :]).then_inc(rr_out, 1)
                    dve.wait_ge(rr_out, least(u))
                    dve.wait_ge(o_done, least(u))
                    nc.vector.tensor_tensor(attn_t[:, at(-1, 4), b * S:(b + 1) * S], o_ps[:, :], r_sum[:, :],
                                            ALU.mult).then_inc(o_out, 1)
                if has(n, 2):
                    for w, (src, done, hi, out, ready) in enumerate((
                            (aux[0], qh_out, q_hihi, q_lo, ql_out), (aux[1], kh_out, k_hilo, k_hilo, kl_out))):
                        for h in (0, 1):
                            dve.wait_ge(done, least(u * 2 + (5 + h)))
                            to = SPLIT[h] if w == 0 else OTHER[h]
                            nc.vector.scalar_tensor_tensor(
                                out=out[to, par, h, :], in0=src[SPLIT[h], :],
                                scalar=bias_pair[SPLIT[h], 0, w:w + 1],
                                in1=hi[SPLIT[h], par, h, :].bitcast(f32), op0=ALU.add, op1=ALU.subtract,
                            ).then_inc(ready, 1)
                if has(n, 1):
                    maxima(u + 1, 1)
                    dve.wait_ge(max_out, least((u + 2) * 6))
                    nc.vector.tensor_scalar(shift[:, :, :, 0], row_max[:, :, :], -1.0, None, ALU.mult).then_inc(sh_hi, 1)
                    dve.wait_ge(sh_hi, least(u + 2))
                    nc.vector.scalar_tensor_tensor(out=shift[:, :, :, 1], in0=row_max[:, :, :], scalar=-1.0,
                                                   in1=shift[:, :, :, 0], op0=ALU.mult,
                                                   op1=ALU.subtract).then_inc(sh_out, 1)
                if has(n, 2):
                    dve.wait_ge(v_done, least(u + 3))
                    nc.vector.tensor_tensor(v_nat[:, (m + 2) % 4, :, :],
                                            aux[0][:, :].rearrange("p (i d) -> p i d", i=NT),
                                            bias_v_pair[:, :].unsqueeze(1).broadcast_to([128, NT, 2 * D]),
                                            ALU.add).then_inc(v_out, 1)

            nc.vector.memset(ones64[:, :], 1.0)
            for t in (k_hi1, q_lo):
                nc.vector.memset(t[:, :, :, :].bitcast(f32), 0.0)
            nc.vector.drain()
            nc.vector.memset(k_hi1[64:66, :, 0, :].bitcast(f32), 1.0)
            nc.vector.memset(k_hi1[0:2, :, 1, :].bitcast(f32), 1.0).then_inc(zeroed, 1)
            dve.wait_ge(x_split, 1)
            nc.vector.tensor_tensor(x_lo[:, :], x_t[:, :], x_hi[:, :].bitcast(f32), ALU.subtract).then_inc(x_split, 1)
            dve.wait_ge(const_in, CONSTS)
            dve.wait_ge(w_split, 1)
            for u in (-2, -1, 0):
                slot(u, u % 4, u, lambda d, c: (u + d) // c)
            with dve.Fori(0, (UNITS - 4) // 4) as p:
                for k in range(1, 5):
                    slot(p * 4 + k, k % 4, None, lambda d, c: p * (4 // c) + (k + d) // c)
            for u in range(UNITS - 3, UNITS + 1):
                slot(u, u % 4, u, lambda d, c: (u + d) // c)

        @block.gpsimd
        def _(pool):
            def split_w(pair):
                pool.wait_ge(w_in, least((pair + 1) * 16))
                pool.wait_ge(v_done, least(pair * 4))
                pool.sem_inc(passed, 1)
                nc.gpsimd.tensor_copy(w_hi[:, :, :], w_pair[:, 0:2, :]).then_inc(w_hi_out, 1)
                pool.wait_ge(w_hi_out, least(pair + 1))
                nc.gpsimd.tensor_tensor(w_lo[:, :, :], w_pair[:, 0:2, :], w_hi[:, :, :].bitcast(f32),
                                        ALU.subtract)
                pool.wait_ge(v_out, least(pair * 4))
                pool.wait_ge(kl_out, least(pair * 8))
                pool.sem_inc(passed, 1)
                nc.gpsimd.tensor_copy(bias_pair[:, 0, :], bias_qk[:, :, pair]) if isinstance(pair, int) else \
                    nc.gpsimd.tensor_copy(bias_pair[:, 0, :], bias_qk[:, :, bass.ds(pair, 1)].rearrange("p a o -> p (a o)"))
                nc.gpsimd.tensor_copy(bias_v_pair[:, :], bias_v[:, pair, :]).then_inc(w_split, 1)

            def slot(u, m, n, at):
                par = m % 2
                if m == 1 and has(n, 2):
                    todo = at(3, 4)
                else:
                    todo = None
                if has(n, 0):
                    for h in (0, 1):
                        pool.wait_ge(exp_out, least(u * 4 + (2 * h + 2)))
                        pool.sem_inc(passed, 1)
                        for at, step in ((0, 512), (1152, 128)):
                            blk = probs[:, par, h, at:at + 2 * step].rearrange("p (j c) -> p j c", j=2)[:, :, 0:T]
                            last = nc.gpsimd.affine_select(out=blk, in_=blk, compare_op=ALU.is_ge, fill=0.0, base=0,
                                                           pattern=[[0, 2], [1, T]], channel_multiplier=-1)
                        last.then_inc(masked, 1)
                if todo is not None and not (n is not None and n + 3 >= UNITS):
                    split_w(todo)

            pool.wait_ge(const_in, CONSTS)
            split_w(0)
            for u in (-2, -1, 0):
                slot(u, u % 4, u, lambda d, c: (u + d) // c)
            with pool.Fori(0, (UNITS - 4) // 4) as p:
                for k in range(1, 5):
                    slot(p * 4 + k, k % 4, None, lambda d, c: p * (4 // c) + (k + d) // c)
            for u in range(UNITS - 3, UNITS + 1):
                slot(u, u % 4, u, lambda d, c: (u + d) // c)

        @block.sync
        def _(sp):
            def load_w(pair):
                sp.dma_start(w_pair[:, :, :], w_qkv[pair, :, :, :]).then_inc(w_in, 16)

            def slot(u, m, n, at):
                par = m % 2
                if has(n, 2):
                    for w, (t, hi, done, out) in enumerate(((q_hihi, qh_out, None, q_dup), (k_hilo, kh_out, k_hi1, k_dup))):
                        for h in (0, 1):
                            sp.wait_ge(hi, least(u * 2 + (5 + h)))
                            if w == 0:
                                sp.dma_start(t[OTHER[h], par, h, :].bitcast(f32), t[SPLIT[h], par, h, :].bitcast(f32)).then_inc(out[par], 16)
                            else:
                                sp.dma_start(k_hi1[SPLIT[h], par, h, :].bitcast(f32), t[SPLIT[h], par, h, :].bitcast(f32)).then_inc(out[par], 16)
                if m == 1 and not (n is not None and n + 3 >= UNITS):
                    sp.wait_ge(v_done, least(u + 3))
                    load_w(at(3, 4))

            sp.dma_start(x_t[:, :], xT).then_inc(x_in, 16)
            load_w(0)
            sp.dma_start(bias_qk[:, :, :], b_qk).then_inc(const_in, 16)
            sp.dma_start(bias_v[:, :, :], b_v).then_inc(const_in, 16)
            sp.dma_start(neg_mask[:, :], causal).then_inc(const_in, 16)
            sp.dma_start(ident_b[:, :], ident).then_inc(const_in, 16)
            for u in (-2, -1, 0):
                slot(u, u % 4, u, lambda d, c: (u + d) // c)
            with sp.Fori(0, (UNITS - 4) // 4) as p:
                for k in range(1, 5):
                    slot(p * 4 + k, k % 4, None, lambda d, c: p * (4 // c) + (k + d) // c)
            for u in range(UNITS - 3, UNITS + 1):
                slot(u, u % 4, u, lambda d, c: (u + d) // c)


HX, DK = 16, 8
C = 77
F = 128
EPS = 1e-5


def rest_of_layer(nc, banks, attn_t, x_nat, wo, b_o, ctx_t, w_x, head_mask, group_mask, ident_f, ident_b_in,
                  ffn_k, scales, ffn_b, out):
    f32, bf16, i32 = mybir.dt.float32, mybir.dt.bfloat16, mybir.dt.int32
    ALU, ACT, AX = mybir.AluOpType, mybir.ActivationFunctionType, mybir.AxisListType
    ctx = ExitStack()
    with ctx:
        sb = lambda name, shape, dt=f32: ctx.enter_context(nc.sbuf_tensor(name, shape, dt))
        sem = lambda name: ctx.enter_context(nc.semaphore(name))
        two = lambda name, shape, dt=f32: [sb(f"{name}{j}", shape, dt) for j in range(2)]

        wo_s = sb("wo_s", [128, PAIRS, E])
        bo_s = sb("bo_s", [128, 1])
        ctx_s = sb("ctx_s", [128, B, C])
        wx_s = sb("wx_s", [128, 4, E])
        hmask = sb("hmask", [128, HX])
        gmask = sb("gmask", [128, 4, 32])
        id_f = sb("id_f", [128, 128])
        id_b = sb("id_b", [128, 128], bf16)
        fk_s = sb("fk_s", [128, F], bf16)
        fkq = sb("fkq", [128, F], bf16)
        sc_s = sb("sc_s", [128, 2])
        sc_r = sb("sc_r", [128, 2])
        sc_p = sb("sc_p", [128, 1])
        fb_s = sb("fb_s", [128, F], bf16)
        gm_c = sb("gm_c", [C, 4, 32])
        halves = sb("halves", [128, NT])
        k2_s = sb("k2_s", [128, B, C])
        v2_s = sb("v2_s", [C, B, E])
        k_heads = two("k_heads", [128, HX, C])
        v_heads = two("v_heads", [C, 4, 4, 32])
        x_s = sb("x_s", [128, B, NT, E])
        y_out = sb("y_out", [128, B, NT, E])
        y_t = two("y_t", [128, S])
        r_s = two("r_s", [128, NT, E])
        stats = two("stats", [128, NT, 6])
        mv = two("mv", [128, NT, 2])
        var_e = two("var_e", [128, NT])
        rstd = two("rstd", [128, NT])
        xn = two("xn", [128, NT, E])
        q2_t = two("q2_t", [128, S])
        mx = two("mx", [128, HX])
        ex = two("ex", [128, HX, C])
        p_t = sb("p_t", [C, HX, S])
        rs2 = two("rs2", [128, S])
        x_b = two("x_b", [128, S], bf16)
        qv = two("qv", [128, S])
        qm = two("qm", [128, S])
        xq = two("xq", [128, S], bf16)
        xq_t = two("xq_t", [128, S], bf16)
        y_b = two("y_b", [128, S], bf16)
        scores = banks[:, 4:8, 0:4 * C].rearrange("p b (h k) -> p b h k", h=4)
        own = [banks[:, 2, :], banks[:, 3, :]]
        tp = [banks[:, 0, :], banks[:, 1, :]]
        tpb = [banks[:, j, 0:S // 2].bitcast(bf16) for j in range(2)]
        PER = 2 * (3 + 4 + 1 + 3 + 1 + 8 + 4)

        (inputs_in, kv_done, kv_out, heads_out, wo_done, wo_out, y_done, var_out, rstd_out, norm_out, xt_done,
         xt_out, q2_done, q2_out, sc_done, sc_out, exp2_out, pt_done, pt_even_out, pt_odd_out, pv_done, o2_out,
         y2_done, quant_out, xqt_done, xqt_out, y3_done, y3_out, link_done, passed2, ffn_k_out, halves_out) = (
            sem(n + "_x") for n in ("""inputs_in kv_done kv_out heads_out wo_done wo_out y_done var_out rstd_out
            norm_out xt_done xt_out q2_done q2_out sc_done sc_out exp2_out pt_done pt_even_out pt_odd_out pv_done
            o2_out y2_done quant_out xqt_done xqt_out y3_done y3_out link_done passed2 ffn_k_out halves_out""").split())

        stored = sem("stored")
        LOADS = 16 * 12
        block = ctx.enter_context(nc.Block())

        @block.sync
        def _(sp):
            for dst, src in ((wo_s[:, :, :], wo), (bo_s[:, :], b_o), (ctx_s[:, :, :], ctx_t), (wx_s[:, :, :], w_x),
                             (hmask[:, :], head_mask), (gmask[:, :, :], group_mask), (id_f[:, :], ident_f),
                             (id_b[:, :], ident_b_in), (fk_s[:, :], ffn_k), (sc_s[:, :], scales), (fb_s[:, :], ffn_b), (x_s[:, :, :, :], x_nat)):
                sp.dma_start(dst, src).then_inc(inputs_in, 16)
            with sp.Fori(0, B // 2) as it:
                for j in (0, 1):
                    n = it * 2 + j
                    sp.wait_ge(norm_out, it * 6 + (4 + j + 1))
                    sp.dma_start(out[n, :, :, :], y_out[:, bass.ds(n, 1), :, :].rearrange("p o i e -> p (o i) e")
                                 ).then_inc(stored, 16)
            sp.wait_ge(stored, 16 * B)

        @block.tensor
        def _(pe):
            mm = nc.tensor.matmul
            pe.wait_ge(inputs_in, LOADS)
            mm(own[0][:, 0:B * C], wx_s[:, 1, :], ctx_s[:, :, :].rearrange("p b k -> p (b k)"),
               start=True, stop=True).then_inc(kv_done, 1)
            for b in range(B):
                last = mm(own[1][0:C, b * E:(b + 1) * E], ctx_s[:, b, :], wx_s[:, 2, :], start=True, stop=True)
            last.then_inc(kv_done, 1)
            pe.wait_ge(kv_out, 2)

            def four(dst, lhs, rhs, done, transpose=False):
                for i in range(NT):
                    sl = slice(i * T, (i + 1) * T)
                    if transpose:
                        last = nc.tensor.transpose(dst[:, sl], lhs(i), rhs)
                    else:
                        last = mm(dst[:, sl], lhs(i), rhs, start=True, stop=True)
                last.then_inc(done, 1)

            with pe.Fori(0, B // 2) as it:
                J = (0, 1)
                n = lambda j: it * 2 + (j + 1)
                for j in J:
                    for p in range(PAIRS):
                        last = mm(own[j], wo_s[:, p, :], attn_t[:, p, bass.ds((it * 2 + j) * S, S)],
                                  start=(p == 0), stop=(p == PAIRS - 1))
                    last.then_inc(wo_done, 1)
                for j in J:
                    pe.wait_ge(wo_out, n(j))
                    four(own[j], lambda i: y_t[j][:, i * T:(i + 1) * T], id_f[:, :], y_done, True)
                for j in J:
                    pe.wait_ge(norm_out, it * 6 + (j + 1))
                    four(own[j], lambda i: xn[j][:, i, :], id_f[:, :], xt_done, True)
                for j in J:
                    pe.wait_ge(xt_out, n(j))
                    mm(own[j], wx_s[:, 0, :], r_s[j][:, :, :].rearrange("p i e -> p (i e)"),
                       start=True, stop=True).then_inc(q2_done, 1)
                for j in J:
                    pe.wait_ge(q2_out, n(j))
                    pe.wait_ge(heads_out, n(j))

                    def score(i):
                        if i + j > 0:
                            pe.wait_ge(sc_out, it * 8 + (4 * j + i))
                        for c in range(4):
                            last = mm(banks[:, 4 + c, 0:4 * C], q2_t[j][:, i * T:(i + 1) * T],
                                      k_heads[j][:, 4 * c:4 * c + 4, :].rearrange("p h k -> p (h k)"),
                                      start=True, stop=True)
                        last.then_inc(sc_done, 1)

                    score(0)
                    for i in range(NT):
                        if i + 1 < NT:
                            score(i + 1)
                        pe.wait_ge(exp2_out, it * 8 + (4 * j + i + 1))
                        for f in range(4):
                            if i + j + f // 2 > 0:
                                pe.wait_ge((pt_even_out, pt_odd_out)[f % 2], it * 16 + (8 * j + 2 * i + f // 2))
                            for h in range(4):
                                last = nc.tensor.transpose(tp[f % 2][0:C, h * T:(h + 1) * T],
                                                           ex[i % 2][:, 4 * f + h, :], id_f[:, :])
                            last.then_inc(pt_done, 1)
                    pe.wait_ge(pt_even_out, it * 16 + (8 * j + 8))
                    pe.wait_ge(pt_odd_out, it * 16 + (8 * j + 8))
                    if j == 1:
                        pe.wait_ge(o2_out, n(0))
                    for dst, lhs in ((own[1 - j], lambda g, a: gm_c[:, a, :]),
                                     (own[j], lambda g, a: v_heads[j][:, g, a, :])):
                        for a in range(4):
                            for g in range(4):
                                last = mm(dst[32 * g:32 * g + 32, :], lhs(g, a), p_t[:, 4 * g + a, :],
                                          start=(a == 0), stop=(a == 3))
                        last.then_inc(pv_done, 1)
                for j in J:
                    pe.wait_ge(o2_out, n(1))
                    four(own[j], lambda i: y_t[j][:, i * T:(i + 1) * T], wx_s[:, 3, :], y2_done)
                for j in J:
                    pe.wait_ge(quant_out, n(j))
                    four(tpb[j], lambda i: xq[j][:, i * T:(i + 1) * T], id_b[:, :], xqt_done, True)
                for j in J:
                    pe.wait_ge(xqt_out, n(j))
                    pe.wait_ge(ffn_k_out, 1)
                    four(own[j], lambda i: xq_t[j][:, i * T:(i + 1) * T], fkq[:, :], y3_done)
                pe.wait_ge(y3_out, n(1))

        @block.scalar
        def _(act):
            copy = nc.scalar.copy
            act.wait_ge(kv_done, 1)
            copy(k2_s[:, :, :].rearrange("p b k -> p (b k)"), own[0][:, 0:B * C]).then_inc(kv_out, 1)
            act.wait_ge(kv_done, 2)
            copy(v2_s[:, :, :].rearrange("p b e -> p (b e)"), own[1][0:C, :]).then_inc(kv_out, 1)
            act.wait_ge(inputs_in, LOADS)
            with act.Fori(0, B // 2) as it:
                J = (0, 1)
                n = lambda j: it * 2 + (j + 1)
                for j in J:
                    act.wait_ge(wo_done, n(j))
                    nc.scalar.activation(y_t[j][:, :], own[j], ACT.Identity, bias=bo_s[:, 0:1]).then_inc(wo_out, 1)
                for j in J:
                    act.wait_ge(xt_done, n(j))
                    copy(r_s[j][:, :, :].rearrange("p i e -> p (i e)"), own[j]).then_inc(xt_out, 1)
                for j in J:
                    act.wait_ge(q2_done, n(j))
                    copy(q2_t[j][:, :], own[j]).then_inc(q2_out, 1)
                for j in J:
                    for i in range(NT):
                        act.wait_ge(sc_out, it * 8 + (4 * j + i + 1))
                        nc.scalar.activation(ex[i % 2][:, :, :], ex[i % 2][:, :, :], ACT.Exp,
                                             scale=DK ** -0.5).then_inc(exp2_out, 1)
                        for f in (0, 2):
                            act.wait_ge(pt_done, it * 32 + (16 * j + 4 * i + f + 1))
                            if j == 1 and i == 0:
                                act.wait_ge(pv_done, it * 4 + 2)
                            copy(p_t[:, 4 * f:4 * f + 4, i * T:(i + 1) * T],
                                 tp[0][0:C, :].rearrange("p (h s) -> p h s", h=4)).then_inc(pt_even_out, 1)
                for j in J:
                    act.wait_ge(xqt_done, n(j))
                    copy(xq_t[j][:, :], tpb[j]).then_inc(xqt_out, 1)
                for j in J:
                    act.wait_ge(y3_done, n(j))
                    act.wait_ge(ffn_k_out, 1)
                    nc.scalar.activation(y_b[j][:, :], own[j], ACT.Copy, scale=sc_p[:, 0:1]).then_inc(y3_out, 1)

        @block.gpsimd
        def _(pool):
            nc.gpsimd.memset(halves[:, :], -0.5).then_inc(halves_out, 1)
            pool.wait_ge(halves_out, 1)
            with pool.Fori(0, B // 2) as it:
                for l in range(3):
                    for j in (0, 1):
                        c = it * 6 + (2 * l + j + 1)
                        pool.wait_ge(var_out, c)
                        nc.gpsimd.tensor_tensor(rstd[j][:, :], var_e[j][:, :], halves[:, :], ALU.pow).then_inc(rstd_out, 1)

        @block.vector
        def _(dve):
            V = nc.vector
            made = [0, None]

            def link(ins):
                made[0] += 1
                ins.then_inc(link_done, 1)
                dve.wait_ge(link_done, made[0] if made[1] is None else made[1] + made[0])
                dve.sem_inc(passed2, 1)

            def quantize(dst, src, scale_r, v, m):
                link(V.tensor_scalar(v, src, scale_r, None, ALU.mult))
                link(V.tensor_single_scalar(m.bitcast(i32), v.bitcast(i32), 0x7F800000, ALU.bitwise_and))
                link(V.tensor_scalar(m, m, 2.0 ** -6, 1.5 * 2 ** 20, ALU.max, ALU.mult))
                link(V.tensor_tensor(v, v, m, ALU.add))
                link(V.tensor_tensor(v, v, m, ALU.subtract))
                link(V.tensor_tensor(m, v, v, ALU.mult))
                link(V.tensor_scalar(m, m, 448.0 ** 2, 3.0e38, ALU.is_gt, ALU.mult))
                link(V.tensor_scalar(m, m, 3.0e38, 0.0, ALU.mult, ALU.mult))
                return V.tensor_tensor(dst, v, m, ALU.add)

            def layernorm(src, j, l, it):
                for i in range(NT):
                    last = V.bn_stats(out=stats[j][:, i, :], in_=src[:, i, :])
                link(last)
                for i in range(NT):
                    last = V.bn_aggr(out=mv[j][:, i, :], in_=stats[j][:, i, :])
                link(last)
                V.tensor_scalar(var_e[j][:, :], mv[j][:, :, 1], EPS, None, ALU.add).then_inc(var_out, 1)

            dve.wait_ge(inputs_in, LOADS)
            V.tensor_copy(gm_c[:, :, :], gmask[0:C, :, :])
            link(V.reciprocal(sc_r[:, :], sc_s[:, :]))
            link(V.tensor_tensor(sc_p[:, :], sc_s[:, 0:1], sc_s[:, 1:2], ALU.mult))
            quantize(fkq[:, :], fk_s[:, :], sc_r[:, 1:2], qv[0][:, 0:F], qm[0][:, 0:F]).then_inc(ffn_k_out, 1)
            dve.wait_ge(kv_out, 2)
            base = made[0]
            with dve.Fori(0, B // 2) as it:
                made[0] = base
                made[1] = it * PER
                J = (0, 1)
                n = lambda j: it * 2 + (j + 1)
                flat = lambda t: t[:, :, :].rearrange("p i e -> p (i e)")
                for j in J:
                    b = it * 2 + j
                    V.tensor_tensor(k_heads[j][:, :, :], k2_s[:, bass.ds(b, 1), :].broadcast_to([128, HX, C]),
                                    hmask[:, :].unsqueeze(2).broadcast_to([128, HX, C]), ALU.mult)
                    for g in range(4):
                        last = V.tensor_tensor(
                            v_heads[j][:, g, :, :],
                            v2_s[:, bass.ds(b, 1), 32 * g:32 * g + 32].broadcast_to([C, 4, 32]),
                            gmask[0:C, :, :], ALU.mult)
                    last.then_inc(heads_out, 1)
                for j in J:
                    dve.wait_ge(y_done, n(j))
                    link(V.tensor_tensor(flat(r_s[j]), own[j],
                                         x_s[:, bass.ds(it * 2 + j, 1), :, :].rearrange("p o i e -> p (o i e)"), ALU.add))
                    layernorm(r_s[j], j, 0, it)
                for j in J:
                    dve.wait_ge(rstd_out, it * 6 + (j + 1))
                    for i in range(NT):
                        last = V.tensor_scalar(xn[j][:, i, :], r_s[j][:, i, :], mv[j][:, i, 0:1], rstd[j][:, i:i + 1],
                                               ALU.subtract, ALU.mult)
                    last.then_inc(norm_out, 1)
                for j in J:
                    for i in range(NT):
                        c = it * 8 + (4 * j + i + 1)
                        dve.wait_ge(sc_done, c)
                        link(V.tensor_reduce(mx[i % 2][:, :].rearrange("p (b h) -> p b h", b=4), scores,
                                             axis=AX.X, op=ALU.max))
                        if 4 * j + i > 1:
                            dve.wait_ge(pt_done, it * 32 + (16 * j + 4 * i - 4))
                        V.tensor_tensor(ex[i % 2][:, :, :].rearrange("p (b h) k -> p b h k", b=4), scores,
                                        mx[i % 2][:, :].rearrange("p (b h) -> p b h", b=4).unsqueeze(3)
                                        .broadcast_to([128, 4, 4, C]), ALU.subtract).then_inc(sc_out, 1)

                        def evacuate(i):
                            for f in (1, 3):
                                dve.wait_ge(pt_done, it * 32 + (16 * j + 4 * i + f + 1))
                                V.tensor_copy(p_t[:, 4 * f:4 * f + 4, i * T:(i + 1) * T],
                                              tp[1][0:C, :].rearrange("p (h s) -> p h s", h=4)).then_inc(pt_odd_out, 1)

                        if i >= 1:
                            evacuate(i - 1)
                    evacuate(NT - 1)
                    dve.wait_ge(pv_done, it * 4 + (2 * j + 1))
                    link(V.reciprocal(rs2[j][:, :], own[1 - j]))
                    dve.wait_ge(pv_done, it * 4 + (2 * j + 2))
                    V.tensor_tensor(y_t[j][:, :], own[j], rs2[j][:, :], ALU.mult).then_inc(o2_out, 1)
                for l in (1, 2):
                    if l == 2:
                        for j in J:
                            link(V.tensor_copy(x_b[j][:, :], flat(xn[j])))
                            quantize(xq[j][:, :], x_b[j][:, :], sc_r[:, 0:1], qv[j][:, :], qm[j][:, :]
                                     ).then_inc(quant_out, 1)
                        for j in J:
                            dve.wait_ge(y3_out, n(j))
                            link(V.tensor_tensor(xq[j][:, :].rearrange("p (i e) -> p i e", i=NT),
                                                 y_b[j][:, :].rearrange("p (i e) -> p i e", i=NT),
                                                 fb_s[:, :].unsqueeze(1).broadcast_to([128, NT, F]), ALU.add))
                            link(V.tensor_tensor(flat(r_s[j]), xq[j][:, :], flat(xn[j]), ALU.add))
                            layernorm(r_s[j], j, l, it)
                    else:
                        for j in J:
                            dve.wait_ge(y2_done, n(j))
                            link(V.tensor_tensor(flat(r_s[j]), own[j], flat(xn[j]), ALU.add))
                            layernorm(r_s[j], j, l, it)
                    for j in J:
                        dve.wait_ge(rstd_out, it * 6 + (2 * l + j + 1))
                        for i in range(NT):
                            dst = xn[j][:, i, :] if l == 1 else y_out[:, bass.ds(it * 2 + j, 1), i, :].rearrange("p o e -> p (o e)")
                            last = V.tensor_scalar(dst, r_s[j][:, i, :], mv[j][:, i, 0:1],
                                                   rstd[j][:, i:i + 1], ALU.subtract, ALU.mult)
                        last.then_inc(norm_out, 1)
                        dve.wait_ge(norm_out, it * 6 + (2 * l + j + 1))
                assert made[0] - base == PER, made[0] - base


_INS = ["xT", "w_qkv", "b_qk", "b_v", "causal", "ident", "x_nat", "wo", "b_o", "ctx_t", "w_x", "head_mask",
        "group_mask", "ident_f", "ffn_k", "scales", "ffn_b"]


def program(nc, a, out):
    ctx = ExitStack()
    with ctx:
        banks = ctx.enter_context(nc.psum_tensor("banks", [128, 8, 512], mybir.dt.float32))
        attn_t = ctx.enter_context(nc.sbuf_tensor("attn_t", [128, PAIRS, B * S], mybir.dt.float32))
        self_attention(nc, banks, attn_t, a["xT"], a["w_qkv"], a["b_qk"], a["b_v"], a["causal"], a["ident"])
        rest_of_layer(nc, banks, attn_t, a["x_nat"], a["wo"], a["b_o"], a["ctx_t"], a["w_x"], a["head_mask"],
                      a["group_mask"], a["ident_f"], a["ident"], a["ffn_k"], a["scales"], a["ffn_b"], out)


def kernel(**inputs):
    import concourse.bacc as bacc
    from concourse.bass_utils import run_bass_kernel_spmd as run

    g = {k: np.asarray(v) for k, v in inputs.items()}
    pairs = lambda w: w.transpose(1, 0, 2).reshape(E, PAIRS, 2 * D).transpose(1, 0, 2)
    x = g["x"]
    bf = g["L0_ffn_kernel"].dtype
    mask = np.zeros((T, S), np.float32)
    mask[:, S - T:] = np.where(np.arange(T)[None] > np.arange(T)[:, None], -3.0e38, 0.0)
    lay = {
        "xT": x.reshape(B * S, E).T,
        "w_qkv": np.stack([pairs(g["L0_attn_W" + n]) for n in "qkv"], 2),
        "b_qk": np.stack([g["L0_attn_b" + n].reshape(PAIRS, 2 * D).T for n in "qk"], 1),
        "b_v": np.broadcast_to(g["L0_attn_bv"].reshape(1, PAIRS, 2 * D), (128, PAIRS, 2 * D)),
        "causal": mask,
        "ident": np.eye(128).astype(bf),
        "x_nat": x.reshape(B, NT, T, E).transpose(2, 0, 1, 3),
        "wo": g["L0_attn_Wo"].reshape(PAIRS, 2 * D, E).transpose(1, 0, 2),
        "b_o": g["L0_attn_bo"].reshape(E, 1),
        "ctx_t": g["ctx_1024"].transpose(2, 0, 1),
        "w_x": np.stack([g["L0_xattn_W" + n].T for n in "qkvo"], 1),
        "head_mask": np.repeat(np.eye(HX, dtype=np.float32), DK, 0),
        "group_mask": np.broadcast_to(np.repeat(np.eye(4, dtype=np.float32), DK, 1), (128, 4, 32)),
        "ident_f": np.eye(128, dtype=np.float32),
        "ffn_k": g["L0_ffn_kernel"],
        "scales": np.broadcast_to(np.stack([g["L0_ffn_input_scale"], g["L0_ffn_kernel_scale"]], 1), (128, 2)),
        "ffn_b": np.broadcast_to(g["L0_ffn_bias"], (128, F)),
    }
    lay = {k: np.ascontiguousarray(v) for k, v in lay.items()}
    nc = bacc.Bacc("TRN2", target_bir_lowering=False, num_devices=1)
    a = {k: nc.dram_tensor(k, lay[k].shape, mybir.dt.from_np(lay[k].dtype), kind="ExternalInput").ap() for k in _INS}
    out = nc.dram_tensor("out", (B, T, NT, E), mybir.dt.float32, kind="ExternalOutput").ap()
    program(nc, a, out)
    r = run(nc, [lay], core_ids=[0])
    return r.results[0]["out"].transpose(0, 2, 1, 3).reshape(B, S, E)
```

```python
import numpy as np
import concourse.bass as bass
from concourse import mybir
from contextlib import ExitStack

B, S, E = 4, 512, 128
H, D = 16, 64
T = 128
NT = S // T
PAIRS = H // 2
UNITS = PAIRS * B


def self_attention(nc, banks, attn_t, xT, w_qkv, b_qk, causal, ident):
    f32, f32r, bf16 = mybir.dt.float32, mybir.dt.float32r, mybir.dt.bfloat16
    ALU, ACT = mybir.AluOpType, mybir.ActivationFunctionType
    ctx = ExitStack()
    with ctx:
        sb = lambda name, shape, dt=f32: ctx.enter_context(nc.sbuf_tensor(name, shape, dt))
        sem = lambda name: ctx.enter_context(nc.semaphore(name))

        x_t = sb("x_t", [128, B * S])
        x_hi = sb("x_hi", [128, B * S], f32r)
        x_lo = sb("x_lo", [128, B * S], f32r)
        w_all = sb("w_all", [128, PAIRS, 3, 2 * D])
        w_hi = sb("w_hi", [128, 2, 2 * D], f32r)
        w_lo = sb("w_lo", [128, 2, 2 * D], f32r)
        bias_qk = sb("bias_qk", [128, 2, PAIRS])
        neg_mask = sb("neg_mask", [128, S])
        ident_b = sb("ident_b", [128, 128], bf16)
        ones64 = sb("ones64", [128, D])
        q_hihi = sb("q_hihi", [128, 2, 2, S], f32r)
        q_lo = sb("q_lo", [128, 2, 2, S], f32r)
        k_hilo = sb("k_hilo", [128, 2, 2, S], f32r)
        k_hi1 = sb("k_hi1", [128, 2, 2, S], f32r)
        v_nat = sb("v_nat", [128, 4, NT, 2 * D])
        row_max = sb("row_max", [128, 2, NT])
        shift = sb("shift", [128, 2, NT, 2], bf16)
        unused = sb("unused", [128, NT, S], bf16)
        probs = sb("probs", [128, 2, 2, 3 * S])
        p_sum = sb("p_sum", [128, 2, 2, S - T])
        ln_sum = sb("ln_sum", [128, S])
        r_near = sb("r_near", [128, S])
        r_err = sb("r_err", [128, S])
        r_neg = sb("r_neg", [128, S])

        aux = [banks[:, 0, :], banks[:, 1, :]]
        sm = [banks[:, 2, :], banks[:, 3, :]]
        st = banks[:, 4:7, :].rearrange("p b c -> p (b c)")
        o_ps = banks[:, 7, :]

        x_in = [sem(f"x_in{b}") for b in range(B)]
        w_in, w_rest_in, const_in = sem("w_in"), sem("w_rest_in"), sem("const_in")
        x_hi_out, x_lo_out, w_hi_out, w_lo_out, filled = (
            sem("x_hi_out"), sem("x_lo_out"), sem("w_hi_out"), sem("w_lo_out"), sem("filled"))
        q_done, k_done, v_done, rows_done = sem("q_done"), sem("k_done"), sem("v_done"), sem("rows_done")
        sm_done, st_done, o_done, r_done = sem("sm_done"), sem("st_done"), sem("o_done"), sem("r_done")
        qh_out, kh_out, s_out, exp_out, v_out = sem("qh_out"), sem("kh_out"), sem("s_out"), sem("exp_out"), sem("v_out")
        ql_out, kl_out, max_out, shift_hi_out, shift_out = (
            sem("ql_out"), sem("kl_out"), sem("max_out"), sem("shift_hi_out"), sem("shift_out"))
        ln_out, near_out, err_out, neg_out, o_out = (
            sem("ln_out"), sem("near_out"), sem("err_out"), sem("neg_out"), sem("o_out"))
        q_dup, k_dup = [[[sem(f"{n}_dup{i}{h}") for h in (0, 1)] for i in (0, 1)] for n in "qk"]
        masked, added, summed, passed = sem("masked"), sem("added"), sem("summed"), sem("passed")
        CONSTS = 16 * 3

        KEYS = {0: (0, 0), 1: (512, 128), 3: (1024, 256), 2: (1280, 256)}
        SPLIT = [slice(0, D), slice(D, 2 * D)]
        OTHER = [slice(D, 2 * D), slice(0, D)]
        LOOPS = (UNITS - 4) // 4
        PEELED = range(4 * LOOPS + 1, UNITS + 1)

        def least(n):
            return max(n, 0) if isinstance(n, int) else n

        def known(u):
            return u, u % 4, lambda d: 0 <= u + d < UNITS, lambda d, c: (u + d) // c

        def looped(p, k):
            return p * 4 + k, k % 4, lambda d: True, lambda d, c: p * (4 // c) + (k + d) // c

        def of(tensor, pair, *rest):
            return tensor[(slice(None), bass.ds(pair, 1)) + rest]

        block = ctx.enter_context(nc.Block())

        @block.tensor
        def _(pe):
            mm = nc.tensor.matmul

            def maxima(v, par, h, pieces):
                for k in pieces:
                    pe.wait_ge(max_out, least(v * 6 + (3 * h + k - 1)))
                    dst = sm[(3 * h + k) % 2]
                    for i, at, n in (((3, 0, 512),), ((2, 0, 384),), ((1, 0, 256), (0, 256, 256)))[k]:
                        last = mm(dst[:, at:at + n], q_hihi[:, par, h, i * T:(i + 1) * T],
                                  k_hilo[:, par, h, 0:n], start=True, stop=True)
                    last.then_inc(sm_done, 1)

            def scores(u, par, h):
                def stacked(j, n, second):
                    at, q0 = KEYS[j]
                    k, q = ((k_hilo, q_hihi), (k_hi1, q_lo))[second]
                    return mm(st[:, at:at + n], k[:, par, h, j * T:(j + 1) * T], q[:, par, h, q0:S],
                              start=not second, stop=second)
                pe.wait_ge(exp_out, least(u * 4 + (2 * h - 1)))
                stacked(0, 512, False)
                stacked(1, 384, False)
                if h == 0:
                    pe.wait_ge(s_out, u * 2 + 2)
                pe.wait_ge(k_dup[par][h], (at(0, 2) + 1) * 16)
                stacked(0, 512, True)
                stacked(1, 384, True).then_inc(st_done, 1)
                pe.wait_ge(exp_out, least(u * 4 + 2 * h))
                for j in (3, 2):
                    stacked(j, 256, False)
                    last = stacked(j, 256, True)
                last.then_inc(st_done, 1)

            at = None

            def slot(u, m, has, at_):
                nonlocal at
                at = at_
                par, nxt = m % 2, (m + 1) % 2
                b = (m + 2) % 4
                xs = slice(b * S, (b + 1) * S)
                if has(-1):
                    pe.wait_ge(masked, u * 2)
                    pe.wait_ge(v_out, u)
                    pe.wait_ge(o_out, least(u - 1))
                    for j in range(NT):
                        src, q0 = KEYS[j]
                        if j == 3:
                            src, q0 = src + T, q0 + T
                        for h in (0, 1):
                            last = mm(o_ps[SPLIT[h], q0:S], v_nat[:, (m - 1) % 4, j, SPLIT[h]],
                                      probs[:, nxt, h, src:src + S - q0], start=(j == 0), stop=(j == NT - 1))
                    last.then_inc(o_done, 1)
                    pe.wait_ge(summed, u * 2)
                    pe.wait_ge(ql_out, min(u * 2 + 4, 2 * UNITS) if isinstance(u, int) else u * 2 + 4)
                    for h in (0, 1):
                        mm(aux[0][SPLIT[h], 0:T], ones64[:, :], probs[:, nxt, h, 0:T], start=True, stop=True)
                    for h in (0, 1):
                        last = mm(aux[0][SPLIT[h], T:S], ones64[:, :], p_sum[:, nxt, h, :], start=True, stop=True)
                    last.then_inc(r_done, 1)
                if has(0):
                    pe.wait_ge(shift_out, u + 1)
                    pe.wait_ge(kl_out, min(u * 2 + 4, 2 * UNITS) if isinstance(u, int) else u * 2 + 4)
                    for h in (0, 1):
                        rows = (slice(64, 66), slice(0, 2))[h]
                        for i in range(NT):
                            last = mm(aux[1][rows, i * T:(i + 1) * T], shift[:, h, i, :], ident_b[:, :],
                                      start=True, stop=True)
                    last.then_inc(rows_done, 1)
                if has(1):
                    pe.wait_ge(q_dup[nxt][0], (at(1, 2) + 1) * 16)
                    pe.wait_ge(kl_out, u * 2 + 3)
                    maxima(u + 1, nxt, 0, (0, 1))
                if has(0):
                    scores(u, par, 0)
                if has(1):
                    maxima(u + 1, nxt, 0, (2,))
                if has(2):
                    pe.wait_ge(s_out, least(u * 2 + 2))
                    if not has(0):
                        pe.wait_ge(kl_out, least(u * 2 + 4))
                    for i in range(NT):
                        last = mm(aux[1][:, i * T:(i + 1) * T], x_t[:, b * S + i * T:b * S + (i + 1) * T],
                                  of(w_all, at(2, 4), 2, slice(None)).rearrange("p o d -> p (o d)"),
                                  start=True, stop=True)
                    last.then_inc(v_done, 1)
                if has(0):
                    scores(u, par, 1)
                if has(1):
                    pe.wait_ge(q_dup[nxt][1], (at(1, 2) + 1) * 16)
                    pe.wait_ge(kl_out, u * 2 + 4)
                    maxima(u + 1, nxt, 1, (0, 1))
                if has(2):
                    if b == 0:
                        pe.wait_ge(w_lo_out, at(2, 4) + 1)
                    if not has(-1):
                        pe.wait_ge(ql_out, least(u * 2 + 4))
                    for w, (done, out, count) in enumerate(((q_done, err_out, u), (k_done, v_out, u + 3))):
                        pe.wait_ge(out, least(count))
                        mm(aux[w], w_hi[:, w, :], x_hi[:, xs], start=True, stop=False)
                        mm(aux[w], w_hi[:, w, :], x_lo[:, xs], start=False, stop=False)
                        mm(aux[w], w_lo[:, w, :], x_hi[:, xs], start=False, stop=True).then_inc(done, 1)
                if has(1):
                    maxima(u + 1, nxt, 1, (2,))

            pe.wait_ge(w_in, 16)
            pe.wait_ge(const_in, CONSTS)
            pe.wait_ge(filled, 2)
            pe.wait_ge(x_lo_out, 1)
            slot(*known(-2))
            pe.wait_ge(x_lo_out, B)
            pe.wait_ge(w_rest_in, 16)
            slot(*known(-1))
            slot(*known(0))
            with pe.Fori(0, LOOPS) as p:
                for k in range(1, 5):
                    slot(*looped(p, k))
            for u in PEELED:
                slot(*known(u))

        @block.scalar
        def _(act):
            act.preload_act_table_set("natural_log_exp_and_others")

            def slot(u, m, has, at):
                par, nxt = m % 2, (m + 1) % 2
                if has(-1):
                    act.wait_ge(r_done, u)
                    nc.scalar.activation(ln_sum[:, :], aux[0], ACT.Ln).then_inc(ln_out, 1)
                if has(0):
                    act.wait_ge(rows_done, u + 1)
                    nc.scalar.copy(q_lo[64:66, par, 0, :], aux[1][64:66, :]).then_inc(s_out, 1)
                    nc.scalar.copy(q_lo[0:2, par, 1, :], aux[1][0:2, :]).then_inc(s_out, 1)
                if has(-1):
                    act.wait_ge(ln_out, u)
                    act.wait_ge(neg_out, least(u - 1))
                    nc.scalar.activation(r_near[:, :], ln_sum[:, :], ACT.Exp, scale=-1.0).then_inc(near_out, 1)

                def exponentials(h):
                    for k, (lo, hi) in enumerate(((0, 896), (1152, 1536))):
                        act.wait_ge(st_done, u * 4 + (2 * h + k + 1))
                        nc.scalar.activation(probs[:, par, h, lo:hi], st[:, lo:hi], ACT.Exp,
                                             scale=D ** -0.5).then_inc(exp_out, 1)

                if has(0):
                    exponentials(0)
                if has(2):
                    act.wait_ge(v_done, u + 3)
                    nc.scalar.copy(v_nat[:, (m + 2) % 4, :, :].rearrange("p i d -> p (i d)"), aux[1]).then_inc(v_out, 1)
                if has(0):
                    exponentials(1)
                if has(2):
                    for w, (done, dst, out) in enumerate(((q_done, q_hihi, qh_out), (k_done, k_hilo, kh_out))):
                        act.wait_ge(done, u + 3)
                        act.sem_inc(passed, 1)
                        for h in (0, 1):
                            nc.scalar.activation(
                                dst[SPLIT[h], par, h, :], aux[w][SPLIT[h], :], ACT.Identity,
                                bias=bias_qk[SPLIT[h], w, bass.ds(at(2, 4), 1)]).then_inc(out, 1)

            for b in range(B):
                act.wait_ge(x_in[b], 16)
                nc.scalar.copy(x_hi[:, b * S:(b + 1) * S], x_t[:, b * S:(b + 1) * S]).then_inc(x_hi_out, 1)
            act.wait_ge(const_in, CONSTS)
            for u in (-2, -1, 0):
                slot(*known(u))
            with act.Fori(0, LOOPS) as p:
                for k in range(1, 5):
                    slot(*looped(p, k))
            for u in PEELED:
                slot(*known(u))

        @block.vector
        def _(dve):
            def maxima(v, h):
                dve.wait_ge(shift_out, least(v))
                dve.wait_ge(max_out, least(v * 6 + 3 * h))
                for k, pieces in enumerate((((3, 0),), ((2, 0),), ((1, 0), (0, 256)))):
                    dve.wait_ge(sm_done, v * 6 + (3 * h + k + 1))
                    dve.sem_inc(passed, 1)
                    for i, src in pieces:
                        n = (i + 1) * T
                        last = nc.vector.tensor_tensor_reduce(
                            out=unused[:, i, 0:n], in0=sm[(3 * h + k) % 2][:, src:src + n],
                            in1=neg_mask[:, S - n:S], scale=1.0, scalar=-3.0e38,
                            op0=ALU.add, op1=ALU.max, accum_out=row_max[:, h, i:i + 1])
                    last.then_inc(max_out, 1)

            def slot(u, m, has, at):
                par, nxt = m % 2, (m + 1) % 2
                if has(1):
                    maxima(u + 1, 0)
                if has(-1):
                    b = (m - 1) % 4
                    dve.wait_ge(near_out, u)
                    dve.wait_ge(neg_out, least(u - 1))
                    nc.vector.tensor_tensor(r_err[:, :], aux[0], r_near[:, :], ALU.mult).then_inc(err_out, 1)
                    dve.wait_ge(err_out, u)
                    dve.wait_ge(o_out, least(u - 1))
                    nc.vector.scalar_tensor_tensor(out=r_neg[:, :], in0=r_err[:, :], scalar=2.0, in1=r_near[:, :],
                                                   op0=ALU.subtract, op1=ALU.mult).then_inc(neg_out, 1)
                    dve.wait_ge(neg_out, u)
                    dve.wait_ge(o_done, u)
                    nc.vector.scalar_tensor_tensor(
                        out=of(attn_t, at(-1, 4), slice(b * S, (b + 1) * S)).rearrange("p o s -> p (o s)"),
                        in0=o_ps, scalar=-1.0, in1=r_neg[:, :], op0=ALU.mult, op1=ALU.mult).then_inc(o_out, 1)
                if has(1):
                    maxima(u + 1, 1)
                    dve.wait_ge(max_out, (u + 2) * 6)
                    nc.vector.tensor_scalar(shift[:, :, :, 0], row_max[:, :, :], -1.0, None,
                                            ALU.mult).then_inc(shift_hi_out, 1)
                    dve.wait_ge(shift_hi_out, u + 2)
                    nc.vector.scalar_tensor_tensor(out=shift[:, :, :, 1], in0=row_max[:, :, :], scalar=-1.0,
                                                   in1=shift[:, :, :, 0], op0=ALU.mult,
                                                   op1=ALU.subtract).then_inc(shift_out, 1)
                if has(2):
                    for w, (ready, hi, out, done) in enumerate(((qh_out, q_hihi, q_lo, ql_out),
                                                                (kh_out, k_hilo, k_hilo, kl_out))):
                        for h in (0, 1):
                            dve.wait_ge(ready, u * 2 + (5 + h))
                            nc.vector.scalar_tensor_tensor(
                                out=out[(SPLIT, OTHER)[w][h], par, h, :], in0=aux[w][SPLIT[h], :],
                                scalar=bias_qk[SPLIT[h], w, bass.ds(at(2, 4), 1)],
                                in1=hi[SPLIT[h], par, h, :].bitcast(f32), op0=ALU.add, op1=ALU.subtract,
                            ).then_inc(done, 1)

            for b in range(B):
                dve.wait_ge(x_hi_out, b + 1)
                xs = slice(b * S, (b + 1) * S)
                nc.vector.tensor_tensor(x_lo[:, xs], x_t[:, xs], x_hi[:, xs].bitcast(f32),
                                        ALU.subtract).then_inc(x_lo_out, 1)
            dve.wait_ge(const_in, CONSTS)
            dve.wait_ge(filled, 2)
            for u in (-2, -1, 0):
                slot(*known(u))
            with dve.Fori(0, LOOPS) as p:
                for k in range(1, 5):
                    slot(*looped(p, k))
            for u in PEELED:
                slot(*known(u))

        @block.gpsimd
        def _(pool):
            def split_w(pair):
                pool.wait_ge(k_done, least(pair * 4))
                pool.sem_inc(passed, 1)
                nc.gpsimd.tensor_copy(w_hi[:, :, :], of(w_all, pair, slice(0, 2), slice(None)).rearrange(
                    "p o w d -> p (o w) d")).then_inc(w_hi_out, 1)
                pool.wait_ge(w_hi_out, pair + 1)
                pool.sem_inc(passed, 1)
                nc.gpsimd.tensor_tensor(w_lo[:, :, :], of(w_all, pair, slice(0, 2), slice(None)).rearrange(
                    "p o w d -> p (o w) d"), w_hi[:, :, :].bitcast(f32), ALU.subtract).then_inc(w_lo_out, 1)

            def slot(u, m, has, at):
                par = m % 2
                if m == 2 and has(2):
                    split_w(at(2, 4))
                if has(0):
                    pool.wait_ge(r_done, least(u - 1))
                    pool.sem_inc(passed, 1)
                    for h in (0, 1):
                        pool.wait_ge(exp_out, u * 4 + (2 * h + 2))
                        pool.sem_inc(passed, 1)
                        for src, step in ((0, 512), (1152, 128)):
                            blk = probs[:, par, h, src:src + 2 * step].rearrange("p (j c) -> p j c", j=2)[:, :, 0:T]
                            last = nc.gpsimd.affine_select(out=blk, in_=blk, compare_op=ALU.is_ge, fill=0.0, base=0,
                                                           pattern=[[0, 2], [1, T]], channel_multiplier=-1)
                        last.then_inc(masked, 1)
                        pool.wait_ge(masked, u * 2 + (h + 1))
                        p, acc = probs[:, par, h, :], p_sum[:, par, h, :]
                        nc.gpsimd.tensor_tensor(acc, p[:, T:S], p[:, 512:896], ALU.add).then_inc(added, 1)
                        pool.wait_ge(added, u * 4 + (2 * h + 1))
                        nc.gpsimd.tensor_tensor(acc[:, T:], acc[:, T:], p[:, 1280:1536], ALU.add).then_inc(added, 1)
                        pool.wait_ge(added, u * 4 + (2 * h + 2))
                        nc.gpsimd.tensor_tensor(acc[:, 2 * T:], acc[:, 2 * T:], p[:, 1152:1280],
                                                ALU.add).then_inc(summed, 1)

            nc.gpsimd.memset(ones64[:, :], 1.0)
            for t in (k_hi1, q_lo):
                nc.gpsimd.memset(t[:, :, :, :].bitcast(f32), 0.0)
            nc.gpsimd.drain()
            nc.gpsimd.memset(k_hi1[64:66, :, 0, :].bitcast(f32), 1.0).then_inc(filled, 1)
            nc.gpsimd.memset(k_hi1[0:2, :, 1, :].bitcast(f32), 1.0).then_inc(filled, 1)
            pool.wait_ge(filled, 2)
            pool.wait_ge(w_in, 16)
            for u in (-2, -1, 0):
                slot(*known(u))
                if u == -2:
                    pool.wait_ge(w_rest_in, 16)
            with pool.Fori(0, LOOPS) as p:
                for k in range(1, 5):
                    slot(*looped(p, k))
            for u in PEELED:
                slot(*known(u))

        @block.sync
        def _(sp):
            def slot(u, m, has, at):
                par = m % 2
                if has(2):
                    for h in (0, 1):
                        sp.wait_ge(qh_out, u * 2 + (5 + h))
                        sp.dma_start(q_hihi[OTHER[h], par, h, :].bitcast(f32),
                                     q_hihi[SPLIT[h], par, h, :].bitcast(f32)).then_inc(q_dup[par][h], 16)
                    for h in (0, 1):
                        sp.wait_ge(kh_out, u * 2 + (5 + h))
                        sp.dma_start(k_hi1[SPLIT[h], par, h, :].bitcast(f32),
                                     k_hilo[SPLIT[h], par, h, :].bitcast(f32)).then_inc(k_dup[par][h], 16)

            sp.dma_start(w_all[:, 0, :, :], w_qkv[:, 0, :, :]).then_inc(w_in, 16)
            for b in range(B):
                sp.dma_start(x_t[:, b * S:(b + 1) * S], xT[:, b * S:(b + 1) * S]).then_inc(x_in[b], 16)
                if b == 0:
                    sp.dma_start(bias_qk[:, :, :], b_qk).then_inc(const_in, 16)
                    sp.dma_start(neg_mask[:, :], causal).then_inc(const_in, 16)
                    sp.dma_start(ident_b[:, :], ident).then_inc(const_in, 16)
            sp.dma_start(w_all[:, 1:, :, :], w_qkv[:, 1:, :, :]).then_inc(w_rest_in, 16)
            sp.wait_ge(filled, 2)
            for u in (-2, -1, 0):
                slot(*known(u))
            with sp.Fori(0, LOOPS) as p:
                for k in range(1, 5):
                    slot(*looped(p, k))
            for u in PEELED:
                slot(*known(u))


HX, DK = 16, 8
C = 77
F = 128
EPS = 1e-5


def rest_of_layer(nc, banks, attn_t, x_nat, wo, b_o, b_v, ctx_t, w_x, head_mask, group_mask, ident_f, ident_b_in,
                  ffn_k, scales, ffn_b, out):
    f32, bf16, i32 = mybir.dt.float32, mybir.dt.bfloat16, mybir.dt.int32
    ALU, ACT, AX = mybir.AluOpType, mybir.ActivationFunctionType, mybir.AxisListType
    ctx = ExitStack()
    with ctx:
        sb = lambda name, shape, dt=f32: ctx.enter_context(nc.sbuf_tensor(name, shape, dt))
        sem = lambda name: ctx.enter_context(nc.semaphore(name))
        two = lambda name, shape, dt=f32: [sb(f"{name}{j}", shape, dt) for j in range(2)]

        wo_s = sb("wo_s", [128, PAIRS, E])
        bo_s = sb("bo_s", [128, 1])
        bv_s = sb("bv_s", [128, PAIRS])
        bias_y = sb("bias_y", [128, 1])
        ctx_s = sb("ctx_s", [128, B, C])
        wx_s = sb("wx_s", [128, 4, E])
        hmask = sb("hmask", [128, HX])
        gmask = sb("gmask", [128, 4, 32])
        id_f = sb("id_f", [128, 128])
        id_b = sb("id_b", [128, 128], bf16)
        fk_s = sb("fk_s", [128, F], bf16)
        fkq = sb("fkq", [128, F], bf16)
        sc_s = sb("sc_s", [128, 2])
        sc_r = sb("sc_r", [128, 2])
        sc_p = sb("sc_p", [128, 1])
        fb_s = sb("fb_s", [128, F], bf16)
        gm_c = sb("gm_c", [C, 4, 32])
        halves = sb("halves", [128, NT])
        k2_s = sb("k2_s", [128, B, C])
        v2_s = sb("v2_s", [C, B, E])
        k_heads = two("k_heads", [128, HX, C])
        v_heads = two("v_heads", [C, 4, 4, 32])
        x_s = sb("x_s", [128, B, NT, E])
        y_out = sb("y_out", [128, B, NT, E])
        y_t = two("y_t", [128, S])
        r_s = two("r_s", [128, NT, E])
        stats = two("stats", [128, NT, 6])
        mv = two("mv", [128, NT, 2])
        var_e = two("var_e", [128, NT])
        rstd = two("rstd", [128, NT])
        xn = two("xn", [128, NT, E])
        q2_t = two("q2_t", [128, S])
        mx = two("mx", [128, HX])
        ex = two("ex", [128, HX, C])
        p_t = sb("p_t", [C, HX, S])
        rs2 = two("rs2", [128, S])
        x_b = two("x_b", [128, S], bf16)
        qv = two("qv", [128, S])
        qm = two("qm", [128, S])
        xq = two("xq", [128, S], bf16)
        xq_t = two("xq_t", [128, S], bf16)
        y_b = two("y_b", [128, S], bf16)
        scores = banks[:, 4:8, 0:4 * C].rearrange("p b (h k) -> p b h k", h=4)
        own = [banks[:, 2, :], banks[:, 3, :]]
        tp = [banks[:, 0, :], banks[:, 1, :]]
        tpb = [banks[:, j, 0:S // 2].bitcast(bf16) for j in range(2)]
        PER = 2 * (3 + 4 + 1 + 3 + 1 + 8 + 4)

        (inputs_in, kv_done, kv_out, heads_out, wo_done, wo_out, y_done, var_out, rstd_out, norm_out, xt_done,
         xt_out, q2_done, q2_out, sc_done, sc_out, exp2_out, pt_done, pt_even_out, pt_odd_out, pv_done, o2_out,
         y2_done, quant_out, xqt_done, xqt_out, y3_done, y3_out, link_done, passed2, ffn_k_out, halves_out) = (
            sem(n + "_x") for n in ("""inputs_in kv_done kv_out heads_out wo_done wo_out y_done var_out rstd_out
            norm_out xt_done xt_out q2_done q2_out sc_done sc_out exp2_out pt_done pt_even_out pt_odd_out pv_done
            o2_out y2_done quant_out xqt_done xqt_out y3_done y3_out link_done passed2 ffn_k_out halves_out""").split())

        stored = sem("stored")
        LOADS = 16 * 13
        block = ctx.enter_context(nc.Block())

        @block.sync
        def _(sp):
            for dst, src in ((wo_s[:, :, :], wo), (bo_s[:, :], b_o), (bv_s[:, :], b_v), (ctx_s[:, :, :], ctx_t), (wx_s[:, :, :], w_x),
                             (hmask[:, :], head_mask), (gmask[:, :, :], group_mask), (id_f[:, :], ident_f),
                             (id_b[:, :], ident_b_in), (fk_s[:, :], ffn_k), (sc_s[:, :], scales), (fb_s[:, :], ffn_b), (x_s[:, :, :, :], x_nat)):
                sp.dma_start(dst, src).then_inc(inputs_in, 16)
            with sp.Fori(0, B // 2) as it:
                for j in (0, 1):
                    n = it * 2 + j
                    sp.wait_ge(norm_out, it * 6 + (4 + j + 1))
                    sp.dma_start(out[n, :, :, :], y_out[:, bass.ds(n, 1), :, :].rearrange("p o i e -> p (o i) e")
                                 ).then_inc(stored, 16)
            sp.wait_ge(stored, 16 * B)

        @block.tensor
        def _(pe):
            mm = nc.tensor.matmul
            pe.wait_ge(inputs_in, LOADS)
            mm(own[0][:, 0:B * C], wx_s[:, 1, :], ctx_s[:, :, :].rearrange("p b k -> p (b k)"),
               start=True, stop=True).then_inc(kv_done, 1)
            for b in range(B):
                last = mm(own[1][0:C, b * E:(b + 1) * E], ctx_s[:, b, :], wx_s[:, 2, :], start=True, stop=True)
            last.then_inc(kv_done, 1)
            for p in range(PAIRS):
                last = mm(tp[0][:, 0:1], wo_s[:, p, :], bv_s[:, p:p + 1], start=(p == 0), stop=(p == PAIRS - 1))
            last.then_inc(kv_done, 1)
            pe.wait_ge(kv_out, 3)

            def four(dst, lhs, rhs, done, transpose=False):
                for i in range(NT):
                    sl = slice(i * T, (i + 1) * T)
                    if transpose:
                        last = nc.tensor.transpose(dst[:, sl], lhs(i), rhs)
                    else:
                        last = mm(dst[:, sl], lhs(i), rhs, start=True, stop=True)
                last.then_inc(done, 1)

            with pe.Fori(0, B // 2) as it:
                J = (0, 1)
                n = lambda j: it * 2 + (j + 1)
                for j in J:
                    for p in range(PAIRS):
                        last = mm(own[j], wo_s[:, p, :], attn_t[:, p, bass.ds((it * 2 + j) * S, S)],
                                  start=(p == 0), stop=(p == PAIRS - 1))
                    last.then_inc(wo_done, 1)
                for j in J:
                    pe.wait_ge(wo_out, n(j))
                    four(own[j], lambda i: y_t[j][:, i * T:(i + 1) * T], id_f[:, :], y_done, True)
                for j in J:
                    pe.wait_ge(norm_out, it * 6 + (j + 1))
                    four(own[j], lambda i: xn[j][:, i, :], id_f[:, :], xt_done, True)
                for j in J:
                    pe.wait_ge(xt_out, n(j))
                    mm(own[j], wx_s[:, 0, :], r_s[j][:, :, :].rearrange("p i e -> p (i e)"),
                       start=True, stop=True).then_inc(q2_done, 1)
                for j in J:
                    pe.wait_ge(q2_out, n(j))
                    pe.wait_ge(heads_out, n(j))

                    def score(i):
                        if i + j > 0:
                            pe.wait_ge(sc_out, it * 8 + (4 * j + i))
                        for c in range(4):
                            last = mm(banks[:, 4 + c, 0:4 * C], q2_t[j][:, i * T:(i + 1) * T],
                                      k_heads[j][:, 4 * c:4 * c + 4, :].rearrange("p h k -> p (h k)"),
                                      start=True, stop=True)
                        last.then_inc(sc_done, 1)

                    score(0)
                    for i in range(NT):
                        if i + 1 < NT:
                            score(i + 1)
                        pe.wait_ge(exp2_out, it * 8 + (4 * j + i + 1))
                        for f in range(4):
                            if i + j + f // 2 > 0:
                                pe.wait_ge((pt_even_out, pt_odd_out)[f % 2], it * 16 + (8 * j + 2 * i + f // 2))
                            for h in range(4):
                                last = nc.tensor.transpose(tp[f % 2][0:C, h * T:(h + 1) * T],
                                                           ex[i % 2][:, 4 * f + h, :], id_f[:, :])
                            last.then_inc(pt_done, 1)
                    pe.wait_ge(pt_even_out, it * 16 + (8 * j + 8))
                    pe.wait_ge(pt_odd_out, it * 16 + (8 * j + 8))
                    if j == 1:
                        pe.wait_ge(o2_out, n(0))
                    for dst, lhs in ((own[1 - j], lambda g, a: gm_c[:, a, :]),
                                     (own[j], lambda g, a: v_heads[j][:, g, a, :])):
                        for a in range(4):
                            for g in range(4):
                                last = mm(dst[32 * g:32 * g + 32, :], lhs(g, a), p_t[:, 4 * g + a, :],
                                          start=(a == 0), stop=(a == 3))
                        last.then_inc(pv_done, 1)
                for j in J:
                    pe.wait_ge(o2_out, n(1))
                    four(own[j], lambda i: y_t[j][:, i * T:(i + 1) * T], wx_s[:, 3, :], y2_done)
                for j in J:
                    pe.wait_ge(quant_out, n(j))
                    four(tpb[j], lambda i: xq[j][:, i * T:(i + 1) * T], id_b[:, :], xqt_done, True)
                for j in J:
                    pe.wait_ge(xqt_out, n(j))
                    pe.wait_ge(ffn_k_out, 1)
                    four(own[j], lambda i: xq_t[j][:, i * T:(i + 1) * T], fkq[:, :], y3_done)
                pe.wait_ge(y3_out, n(1))

        @block.scalar
        def _(act):
            copy = nc.scalar.copy
            act.wait_ge(kv_done, 1)
            copy(k2_s[:, :, :].rearrange("p b k -> p (b k)"), own[0][:, 0:B * C]).then_inc(kv_out, 1)
            act.wait_ge(kv_done, 2)
            copy(v2_s[:, :, :].rearrange("p b e -> p (b e)"), own[1][0:C, :]).then_inc(kv_out, 1)
            act.wait_ge(inputs_in, LOADS)
            act.wait_ge(kv_done, 3)
            nc.scalar.activation(bias_y[:, :], tp[0][:, 0:1], ACT.Identity, bias=bo_s[:, 0:1]).then_inc(kv_out, 1)
            act.wait_ge(kv_out, 3)
            with act.Fori(0, B // 2) as it:
                J = (0, 1)
                n = lambda j: it * 2 + (j + 1)
                for j in J:
                    act.wait_ge(wo_done, n(j))
                    nc.scalar.activation(y_t[j][:, :], own[j], ACT.Identity, bias=bias_y[:, 0:1]).then_inc(wo_out, 1)
                for j in J:
                    act.wait_ge(xt_done, n(j))
                    copy(r_s[j][:, :, :].rearrange("p i e -> p (i e)"), own[j]).then_inc(xt_out, 1)
                for j in J:
                    act.wait_ge(q2_done, n(j))
                    copy(q2_t[j][:, :], own[j]).then_inc(q2_out, 1)
                for j in J:
                    for i in range(NT):
                        act.wait_ge(sc_out, it * 8 + (4 * j + i + 1))
                        nc.scalar.activation(ex[i % 2][:, :, :], ex[i % 2][:, :, :], ACT.Exp,
                                             scale=DK ** -0.5).then_inc(exp2_out, 1)
                        for f in (0, 2):
                            act.wait_ge(pt_done, it * 32 + (16 * j + 4 * i + f + 1))
                            if j == 1 and i == 0:
                                act.wait_ge(pv_done, it * 4 + 2)
                            copy(p_t[:, 4 * f:4 * f + 4, i * T:(i + 1) * T],
                                 tp[0][0:C, :].rearrange("p (h s) -> p h s", h=4)).then_inc(pt_even_out, 1)
                for j in J:
                    act.wait_ge(xqt_done, n(j))
                    copy(xq_t[j][:, :], tpb[j]).then_inc(xqt_out, 1)
                for j in J:
                    act.wait_ge(y3_done, n(j))
                    act.wait_ge(ffn_k_out, 1)
                    nc.scalar.activation(y_b[j][:, :], own[j], ACT.Copy, scale=sc_p[:, 0:1]).then_inc(y3_out, 1)

        @block.gpsimd
        def _(pool):
            nc.gpsimd.memset(halves[:, :], -0.5).then_inc(halves_out, 1)
            pool.wait_ge(halves_out, 1)
            with pool.Fori(0, B // 2) as it:
                for l in range(3):
                    for j in (0, 1):
                        c = it * 6 + (2 * l + j + 1)
                        pool.wait_ge(var_out, c)
                        nc.gpsimd.tensor_tensor(rstd[j][:, :], var_e[j][:, :], halves[:, :], ALU.pow).then_inc(rstd_out, 1)

        @block.vector
        def _(dve):
            V = nc.vector
            made = [0, None]

            def link(ins):
                made[0] += 1
                ins.then_inc(link_done, 1)
                dve.wait_ge(link_done, made[0] if made[1] is None else made[1] + made[0])
                dve.sem_inc(passed2, 1)

            def quantize(dst, src, scale_r, v, m):
                link(V.tensor_scalar(v, src, scale_r, None, ALU.mult))
                link(V.tensor_single_scalar(m.bitcast(i32), v.bitcast(i32), 0x7F800000, ALU.bitwise_and))
                link(V.tensor_scalar(m, m, 2.0 ** -6, 1.5 * 2 ** 20, ALU.max, ALU.mult))
                link(V.tensor_tensor(v, v, m, ALU.add))
                link(V.tensor_tensor(v, v, m, ALU.subtract))
                link(V.tensor_tensor(m, v, v, ALU.mult))
                link(V.tensor_scalar(m, m, 448.0 ** 2, 3.0e38, ALU.is_gt, ALU.mult))
                link(V.tensor_scalar(m, m, 3.0e38, 0.0, ALU.mult, ALU.mult))
                return V.tensor_tensor(dst, v, m, ALU.add)

            def layernorm(src, j, l, it):
                for i in range(NT):
                    last = V.bn_stats(out=stats[j][:, i, :], in_=src[:, i, :])
                link(last)
                for i in range(NT):
                    last = V.bn_aggr(out=mv[j][:, i, :], in_=stats[j][:, i, :])
                link(last)
                V.tensor_scalar(var_e[j][:, :], mv[j][:, :, 1], EPS, None, ALU.add).then_inc(var_out, 1)

            dve.wait_ge(inputs_in, LOADS)
            V.tensor_copy(gm_c[:, :, :], gmask[0:C, :, :])
            link(V.reciprocal(sc_r[:, :], sc_s[:, :]))
            link(V.tensor_tensor(sc_p[:, :], sc_s[:, 0:1], sc_s[:, 1:2], ALU.mult))
            quantize(fkq[:, :], fk_s[:, :], sc_r[:, 1:2], qv[0][:, 0:F], qm[0][:, 0:F]).then_inc(ffn_k_out, 1)
            dve.wait_ge(kv_out, 2)
            base = made[0]
            with dve.Fori(0, B // 2) as it:
                made[0] = base
                made[1] = it * PER
                J = (0, 1)
                n = lambda j: it * 2 + (j + 1)
                flat = lambda t: t[:, :, :].rearrange("p i e -> p (i e)")
                for j in J:
                    b = it * 2 + j
                    V.tensor_tensor(k_heads[j][:, :, :], k2_s[:, bass.ds(b, 1), :].broadcast_to([128, HX, C]),
                                    hmask[:, :].unsqueeze(2).broadcast_to([128, HX, C]), ALU.mult)
                    for g in range(4):
                        last = V.tensor_tensor(
                            v_heads[j][:, g, :, :],
                            v2_s[:, bass.ds(b, 1), 32 * g:32 * g + 32].broadcast_to([C, 4, 32]),
                            gmask[0:C, :, :], ALU.mult)
                    last.then_inc(heads_out, 1)
                for j in J:
                    dve.wait_ge(y_done, n(j))
                    link(V.tensor_tensor(flat(r_s[j]), own[j],
                                         x_s[:, bass.ds(it * 2 + j, 1), :, :].rearrange("p o i e -> p (o i e)"), ALU.add))
                    layernorm(r_s[j], j, 0, it)
                for j in J:
                    dve.wait_ge(rstd_out, it * 6 + (j + 1))
                    for i in range(NT):
                        last = V.tensor_scalar(xn[j][:, i, :], r_s[j][:, i, :], mv[j][:, i, 0:1], rstd[j][:, i:i + 1],
                                               ALU.subtract, ALU.mult)
                    last.then_inc(norm_out, 1)
                for j in J:
                    for i in range(NT):
                        c = it * 8 + (4 * j + i + 1)
                        dve.wait_ge(sc_done, c)
                        link(V.tensor_reduce(mx[i % 2][:, :].rearrange("p (b h) -> p b h", b=4), scores,
                                             axis=AX.X, op=ALU.max))
                        if 4 * j + i > 1:
                            dve.wait_ge(pt_done, it * 32 + (16 * j + 4 * i - 4))
                        V.tensor_tensor(ex[i % 2][:, :, :].rearrange("p (b h) k -> p b h k", b=4), scores,
                                        mx[i % 2][:, :].rearrange("p (b h) -> p b h", b=4).unsqueeze(3)
                                        .broadcast_to([128, 4, 4, C]), ALU.subtract).then_inc(sc_out, 1)

                        def evacuate(i):
                            for f in (1, 3):
                                dve.wait_ge(pt_done, it * 32 + (16 * j + 4 * i + f + 1))
                                V.tensor_copy(p_t[:, 4 * f:4 * f + 4, i * T:(i + 1) * T],
                                              tp[1][0:C, :].rearrange("p (h s) -> p h s", h=4)).then_inc(pt_odd_out, 1)

                        if i >= 1:
                            evacuate(i - 1)
                    evacuate(NT - 1)
                    dve.wait_ge(pv_done, it * 4 + (2 * j + 1))
                    link(V.reciprocal(rs2[j][:, :], own[1 - j]))
                    dve.wait_ge(pv_done, it * 4 + (2 * j + 2))
                    V.tensor_tensor(y_t[j][:, :], own[j], rs2[j][:, :], ALU.mult).then_inc(o2_out, 1)
                for l in (1, 2):
                    if l == 2:
                        for j in J:
                            link(V.tensor_copy(x_b[j][:, :], flat(xn[j])))
                            quantize(xq[j][:, :], x_b[j][:, :], sc_r[:, 0:1], qv[j][:, :], qm[j][:, :]
                                     ).then_inc(quant_out, 1)
                        for j in J:
                            dve.wait_ge(y3_out, n(j))
                            link(V.tensor_tensor(xq[j][:, :].rearrange("p (i e) -> p i e", i=NT),
                                                 y_b[j][:, :].rearrange("p (i e) -> p i e", i=NT),
                                                 fb_s[:, :].unsqueeze(1).broadcast_to([128, NT, F]), ALU.add))
                            link(V.tensor_tensor(flat(r_s[j]), xq[j][:, :], flat(xn[j]), ALU.add))
                            layernorm(r_s[j], j, l, it)
                    else:
                        for j in J:
                            dve.wait_ge(y2_done, n(j))
                            link(V.tensor_tensor(flat(r_s[j]), own[j], flat(xn[j]), ALU.add))
                            layernorm(r_s[j], j, l, it)
                    for j in J:
                        dve.wait_ge(rstd_out, it * 6 + (2 * l + j + 1))
                        for i in range(NT):
                            dst = xn[j][:, i, :] if l == 1 else y_out[:, bass.ds(it * 2 + j, 1), i, :].rearrange("p o e -> p (o e)")
                            last = V.tensor_scalar(dst, r_s[j][:, i, :], mv[j][:, i, 0:1],
                                                   rstd[j][:, i:i + 1], ALU.subtract, ALU.mult)
                        last.then_inc(norm_out, 1)
                        dve.wait_ge(norm_out, it * 6 + (2 * l + j + 1))
                assert made[0] - base == PER, made[0] - base


_INS = ["xT", "w_qkv", "b_qk", "b_v", "causal", "ident", "x_nat", "wo", "b_o", "ctx_t", "w_x", "head_mask",
        "group_mask", "ident_f", "ffn_k", "scales", "ffn_b"]


def program(nc, a, out):
    ctx = ExitStack()
    with ctx:
        banks = ctx.enter_context(nc.psum_tensor("banks", [128, 8, 512], mybir.dt.float32))
        attn_t = ctx.enter_context(nc.sbuf_tensor("attn_t", [128, PAIRS, B * S], mybir.dt.float32))
        self_attention(nc, banks, attn_t, a["xT"], a["w_qkv"], a["b_qk"], a["causal"], a["ident"])
        rest_of_layer(nc, banks, attn_t, a["x_nat"], a["wo"], a["b_o"], a["b_v"], a["ctx_t"], a["w_x"], a["head_mask"],
                      a["group_mask"], a["ident_f"], a["ident"], a["ffn_k"], a["scales"], a["ffn_b"], out)


def kernel(**inputs):
    import concourse.bacc as bacc
    from concourse.bass_utils import run_bass_kernel_spmd as run

    g = {k: np.asarray(v) for k, v in inputs.items()}
    pairs = lambda w: w.transpose(1, 0, 2).reshape(E, PAIRS, 2 * D).transpose(1, 0, 2)
    x = g["x"]
    bf = g["L0_ffn_kernel"].dtype
    mask = np.zeros((T, S), np.float32)
    mask[:, S - T:] = np.where(np.arange(T)[None] > np.arange(T)[:, None], -3.0e38, 0.0)
    lay = {
        "xT": x.reshape(B * S, E).T,
        "w_qkv": np.stack([pairs(g["L0_attn_W" + n]) for n in "qkv"], 2).transpose(1, 0, 2, 3),
        "b_qk": np.stack([g["L0_attn_b" + n].reshape(PAIRS, 2 * D).T for n in "qk"], 1),
        "b_v": g["L0_attn_bv"].reshape(PAIRS, 2 * D).T,
        "causal": mask,
        "ident": np.eye(128).astype(bf),
        "x_nat": x.reshape(B, NT, T, E).transpose(2, 0, 1, 3),
        "wo": g["L0_attn_Wo"].reshape(PAIRS, 2 * D, E).transpose(1, 0, 2),
        "b_o": g["L0_attn_bo"].reshape(E, 1),
        "ctx_t": g["ctx_1024"].transpose(2, 0, 1),
        "w_x": np.stack([g["L0_xattn_W" + n].T for n in "qkvo"], 1),
        "head_mask": np.repeat(np.eye(HX, dtype=np.float32), DK, 0),
        "group_mask": np.broadcast_to(np.repeat(np.eye(4, dtype=np.float32), DK, 1), (128, 4, 32)),
        "ident_f": np.eye(128, dtype=np.float32),
        "ffn_k": g["L0_ffn_kernel"],
        "scales": np.broadcast_to(np.stack([g["L0_ffn_input_scale"], g["L0_ffn_kernel_scale"]], 1), (128, 2)),
        "ffn_b": np.broadcast_to(g["L0_ffn_bias"], (128, F)),
    }
    lay = {k: np.ascontiguousarray(v) for k, v in lay.items()}
    nc = bacc.Bacc("TRN2", target_bir_lowering=False, num_devices=1)
    a = {k: nc.dram_tensor(k, lay[k].shape, mybir.dt.from_np(lay[k].dtype), kind="ExternalInput").ap() for k in _INS}
    out = nc.dram_tensor("out", (B, T, NT, E), mybir.dt.float32, kind="ExternalOutput").ap()
    program(nc, a, out)
    r = run(nc, [lay], core_ids=[0])
    return r.results[0]["out"].transpose(0, 2, 1, 3).reshape(B, S, E)
```

```python
import numpy as np
import concourse.bass as bass
from concourse import mybir
from contextlib import ExitStack

B, S, E = 4, 512, 128
H, D = 16, 64
T = 128
NT = S // T
PAIRS = H // 2
UNITS = PAIRS * B


def self_attention(nc, banks, attn_t, xT, w_qkv, b_qk, causal, ident, later, later_in):
    f32, f32r, bf16 = mybir.dt.float32, mybir.dt.float32r, mybir.dt.bfloat16
    ALU, ACT = mybir.AluOpType, mybir.ActivationFunctionType
    ctx = ExitStack()
    with ctx:
        sb = lambda name, shape, dt=f32: ctx.enter_context(nc.sbuf_tensor(name, shape, dt))
        sem = lambda name: ctx.enter_context(nc.semaphore(name))

        x_t = sb("x_t", [128, B * S])
        x_hi = sb("x_hi", [128, B * S], f32r)
        x_lo = sb("x_lo", [128, B * S], f32r)
        w_all = sb("w_all", [128, PAIRS, 3, 2 * D])
        w_hi = sb("w_hi", [128, 2, 2 * D], f32r)
        w_lo = sb("w_lo", [128, 2, 2 * D], f32r)
        bias_qk = sb("bias_qk", [128, 2, PAIRS])
        neg_mask = sb("neg_mask", [128, S])
        ident_b = sb("ident_b", [128, 128], bf16)
        ones64 = sb("ones64", [128, D])
        q_hihi = sb("q_hihi", [128, 2, 2, S], f32r)
        q_lo = sb("q_lo", [128, 2, 2, S], f32r)
        k_hilo = sb("k_hilo", [128, 2, 2, S], f32r)
        k_hi1 = sb("k_hi1", [128, 2, 2, S], f32r)
        v_nat = sb("v_nat", [128, 4, NT, 2 * D])
        row_max = sb("row_max", [128, 2, NT])
        shift = sb("shift", [128, 2, NT, 2], bf16)
        unused = sb("unused", [128, NT, S], bf16)
        probs = sb("probs", [128, 2, 2, 3 * S])
        p_sum = sb("p_sum", [128, 2, 2, S - T])
        ln_sum = sb("ln_sum", [128, S])
        r_near = sb("r_near", [128, S])
        r_err = sb("r_err", [128, S])
        r_neg = sb("r_neg", [128, S])

        aux = [banks[:, 0, :], banks[:, 1, :]]
        sm = [banks[:, 2, :], banks[:, 3, :]]
        st = banks[:, 4:7, :].rearrange("p b c -> p (b c)")
        o_ps = banks[:, 7, :]
        max_rows = banks[:, 6, :]

        x_in = [sem(f"x_in{b}") for b in range(B)]
        w_in, w_rest_in, const_in = sem("w_in"), sem("w_rest_in"), sem("const_in")
        x_hi_out, x_lo_out, w_hi_out, w_lo_out, filled = (
            sem("x_hi_out"), sem("x_lo_out"), sem("w_hi_out"), sem("w_lo_out"), sem("filled"))
        q_done, k_done, v_done, rows_done = sem("q_done"), sem("k_done"), sem("v_done"), sem("rows_done")
        sm_done, st_done, o_done, r_done = sem("sm_done"), sem("st_done"), sem("o_done"), sem("r_done")
        qh_out, kh_out, s_out, exp_out, v_out = sem("qh_out"), sem("kh_out"), sem("s_out"), sem("exp_out"), sem("v_out")
        ql_out, kl_out, max_out, shift_hi_out, shift_out = (
            sem("ql_out"), sem("kl_out"), sem("max_out"), sem("shift_hi_out"), sem("shift_out"))
        ln_out, near_out, err_out, neg_out, o_out = (
            sem("ln_out"), sem("near_out"), sem("err_out"), sem("neg_out"), sem("o_out"))
        q_dup, k_dup = [[[sem(f"{n}_dup{i}{h}") for h in (0, 1)] for i in (0, 1)] for n in "qk"]
        masked, added, summed, passed = sem("masked"), sem("added"), sem("summed"), sem("passed")
        CONSTS = 16 * 3

        KEYS = {0: (0, 0), 1: (512, 128), 3: (1024, 256), 2: (1280, 256)}
        SPLIT = [slice(0, D), slice(D, 2 * D)]
        OTHER = [slice(D, 2 * D), slice(0, D)]
        LOOPS = (UNITS - 4) // 4
        PEELED = range(4 * LOOPS + 1, UNITS + 1)

        def least(n):
            return max(n, 0) if isinstance(n, int) else n

        def known(u):
            return u, u % 4, lambda d: 0 <= u + d < UNITS, lambda d, c: (u + d) // c

        def looped(p, k):
            return p * 4 + k, k % 4, lambda d: True, lambda d, c: p * (4 // c) + (k + d) // c

        def of(tensor, pair, *rest):
            return tensor[(slice(None), bass.ds(pair, 1)) + rest]

        block = ctx.enter_context(nc.Block())

        @block.tensor
        def _(pe):
            mm = nc.tensor.matmul

            def maxima(v, par, h, pieces):
                for k in pieces:
                    pe.wait_ge(max_out, least(v * 6 + (3 * h + k - 1)))
                    dst = sm[(3 * h + k) % 2]
                    for i, at, n in (((3, 0, 512),), ((2, 0, 384),), ((1, 0, 256), (0, 256, 256)))[k]:
                        last = mm(dst[:, at:at + n], q_hihi[:, par, h, i * T:(i + 1) * T],
                                  k_hilo[:, par, h, 0:n], start=True, stop=True)
                    last.then_inc(sm_done, 1)

            def sums(u, other):
                pe.wait_ge(summed, u * 2)
                pe.wait_ge(ql_out, min(u * 2 + 4, 2 * UNITS) if isinstance(u, int) else u * 2 + 4)
                for h in (0, 1):
                    mm(aux[0][SPLIT[h], 0:T], ones64[:, :], probs[:, other, h, 0:T], start=True, stop=True)
                for h in (0, 1):
                    last = mm(aux[0][SPLIT[h], T:S], ones64[:, :], p_sum[:, other, h, :], start=True, stop=True)
                last.then_inc(r_done, 1)

            def scores(u, par, h, with_sums):
                def stacked(j, n, second):
                    at, q0 = KEYS[j]
                    k, q = ((k_hilo, q_hihi), (k_hi1, q_lo))[second]
                    return mm(st[:, at:at + n], k[:, par, h, j * T:(j + 1) * T], q[:, par, h, q0:S],
                              start=not second, stop=second)
                pe.wait_ge(exp_out, least(u * 4 + (2 * h - 1)))
                stacked(0, 512, False)
                stacked(1, 384, False)
                if with_sums:
                    sums(u, 1 - par)
                if h == 0:
                    pe.wait_ge(s_out, u * 2 + 2)
                pe.wait_ge(k_dup[par][h], (at(0, 2) + 1) * 16)
                stacked(0, 512, True)
                stacked(1, 384, True).then_inc(st_done, 1)
                pe.wait_ge(exp_out, least(u * 4 + 2 * h))
                for j in (3, 2):
                    stacked(j, 256, False)
                    last = stacked(j, 256, True)
                last.then_inc(st_done, 1)

            at = None

            def slot(u, m, has, at_):
                nonlocal at
                at = at_
                par, nxt = m % 2, (m + 1) % 2
                b = (m + 2) % 4
                xs = slice(b * S, (b + 1) * S)
                if has(-1):
                    pe.wait_ge(masked, u * 2)
                    pe.wait_ge(v_out, u)
                    pe.wait_ge(o_out, least(u - 1))
                    for j in range(NT):
                        src, q0 = KEYS[j]
                        if j == 3:
                            src, q0 = src + T, q0 + T
                        for h in (0, 1):
                            last = mm(o_ps[SPLIT[h], q0:S], v_nat[:, (m - 1) % 4, j, SPLIT[h]],
                                      probs[:, nxt, h, src:src + S - q0], start=(j == 0), stop=(j == NT - 1))
                    last.then_inc(o_done, 1)
                if has(0):
                    pe.wait_ge(shift_out, u + 1)
                    pe.wait_ge(exp_out, least(u * 4))
                    for h in (0, 1):
                        rows = (slice(64, 66), slice(0, 2))[h]
                        for i in range(NT):
                            last = mm(max_rows[rows, i * T:(i + 1) * T], shift[:, h, i, :], ident_b[:, :],
                                      start=True, stop=True)
                    last.then_inc(rows_done, 1)
                if has(1):
                    pe.wait_ge(q_dup[nxt][0], (at(1, 2) + 1) * 16)
                    pe.wait_ge(kl_out, u * 2 + 3)
                    maxima(u + 1, nxt, 0, (0, 1))
                if has(-1) and not has(0):
                    sums(u, nxt)
                if has(0):
                    scores(u, par, 0, has(-1))
                if has(1):
                    maxima(u + 1, nxt, 0, (2,))
                if has(2):
                    pe.wait_ge(kl_out, least(u * 2 + 4))
                    for i in range(NT):
                        last = mm(aux[1][:, i * T:(i + 1) * T], x_t[:, b * S + i * T:b * S + (i + 1) * T],
                                  of(w_all, at(2, 4), 2, slice(None)).rearrange("p o d -> p (o d)"),
                                  start=True, stop=True)
                    last.then_inc(v_done, 1)
                if has(0):
                    scores(u, par, 1, False)
                if has(1):
                    pe.wait_ge(q_dup[nxt][1], (at(1, 2) + 1) * 16)
                    pe.wait_ge(kl_out, u * 2 + 4)
                    maxima(u + 1, nxt, 1, (0, 1))
                if has(2):
                    if b == 0:
                        pe.wait_ge(w_lo_out, at(2, 4) + 1)
                    if not has(-1):
                        pe.wait_ge(ql_out, least(u * 2 + 4))
                    for w, (done, out, count) in enumerate(((q_done, err_out, u), (k_done, v_out, u + 3))):
                        pe.wait_ge(out, least(count))
                        mm(aux[w], w_hi[:, w, :], x_hi[:, xs], start=True, stop=False)
                        mm(aux[w], w_hi[:, w, :], x_lo[:, xs], start=False, stop=False)
                        mm(aux[w], w_lo[:, w, :], x_hi[:, xs], start=False, stop=True).then_inc(done, 1)
                if has(1):
                    maxima(u + 1, nxt, 1, (2,))

            pe.wait_ge(w_in, 16)
            pe.wait_ge(const_in, CONSTS)
            pe.wait_ge(filled, 2)
            pe.wait_ge(x_lo_out, 1)
            slot(*known(-2))
            pe.wait_ge(x_lo_out, B)
            pe.wait_ge(w_rest_in, 16)
            slot(*known(-1))
            slot(*known(0))
            with pe.Fori(0, LOOPS) as p:
                for k in range(1, 5):
                    slot(*looped(p, k))
            for u in PEELED:
                slot(*known(u))

        @block.scalar
        def _(act):
            act.preload_act_table_set("natural_log_exp_and_others")

            def slot(u, m, has, at):
                par, nxt = m % 2, (m + 1) % 2
                if has(0):
                    act.wait_ge(rows_done, u + 1)
                    nc.scalar.copy(q_lo[64:66, par, 0, :], max_rows[64:66, :]).then_inc(s_out, 1)
                    nc.scalar.copy(q_lo[0:2, par, 1, :], max_rows[0:2, :]).then_inc(s_out, 1)
                if has(-1):
                    act.wait_ge(r_done, u)
                    nc.scalar.activation(ln_sum[:, :], aux[0], ACT.Ln).then_inc(ln_out, 1)

                def exponentials(h):
                    for k, (lo, hi) in enumerate(((0, 896), (1152, 1536))):
                        act.wait_ge(st_done, u * 4 + (2 * h + k + 1))
                        nc.scalar.activation(probs[:, par, h, lo:hi], st[:, lo:hi], ACT.Exp,
                                             scale=D ** -0.5).then_inc(exp_out, 1)

                if has(0):
                    exponentials(0)
                if has(-1):
                    act.wait_ge(ln_out, u)
                    act.wait_ge(neg_out, least(u - 1))
                    nc.scalar.activation(r_near[:, :], ln_sum[:, :], ACT.Exp, scale=-1.0).then_inc(near_out, 1)
                if has(2):
                    act.wait_ge(v_done, u + 3)
                    nc.scalar.copy(v_nat[:, (m + 2) % 4, :, :].rearrange("p i d -> p (i d)"), aux[1]).then_inc(v_out, 1)
                if has(0):
                    exponentials(1)
                if has(2):
                    for w, (done, dst, out) in enumerate(((q_done, q_hihi, qh_out), (k_done, k_hilo, kh_out))):
                        act.wait_ge(done, u + 3)
                        act.sem_inc(passed, 1)
                        for h in (0, 1):
                            nc.scalar.activation(
                                dst[SPLIT[h], par, h, :], aux[w][SPLIT[h], :], ACT.Identity,
                                bias=bias_qk[SPLIT[h], w, bass.ds(at(2, 4), 1)]).then_inc(out, 1)

            for b in range(B):
                act.wait_ge(x_in[b], 16)
                nc.scalar.copy(x_hi[:, b * S:(b + 1) * S], x_t[:, b * S:(b + 1) * S]).then_inc(x_hi_out, 1)
            act.wait_ge(const_in, CONSTS)
            for u in (-2, -1, 0):
                slot(*known(u))
            with act.Fori(0, LOOPS) as p:
                for k in range(1, 5):
                    slot(*looped(p, k))
            for u in PEELED:
                slot(*known(u))

        @block.vector
        def _(dve):
            def maxima(v, h, ks):
                if ks[0] == 0:
                    dve.wait_ge(shift_out, least(v))
                    dve.wait_ge(max_out, least(v * 6 + 3 * h))
                for k in ks:
                    dve.wait_ge(sm_done, v * 6 + (3 * h + k + 1))
                    dve.sem_inc(passed, 1)
                    for i, src in (((3, 0),), ((2, 0),), ((1, 0), (0, 256)))[k]:
                        n = (i + 1) * T
                        last = nc.vector.tensor_tensor_reduce(
                            out=unused[:, i, 0:n], in0=sm[(3 * h + k) % 2][:, src:src + n],
                            in1=neg_mask[:, S - n:S], scale=1.0, scalar=-3.0e38,
                            op0=ALU.add, op1=ALU.max, accum_out=row_max[:, h, i:i + 1])
                    last.then_inc(max_out, 1)

            def slot(u, m, has, at):
                par, nxt = m % 2, (m + 1) % 2
                if has(1):
                    maxima(u + 1, 0, (0, 1, 2))
                if has(-1):
                    b = (m - 1) % 4
                    dve.wait_ge(near_out, u)
                    dve.wait_ge(neg_out, least(u - 1))
                    nc.vector.tensor_tensor(r_err[:, :], aux[0], r_near[:, :], ALU.mult).then_inc(err_out, 1)
                    dve.wait_ge(err_out, u)
                    dve.wait_ge(o_out, least(u - 1))
                    nc.vector.scalar_tensor_tensor(out=r_neg[:, :], in0=r_err[:, :], scalar=2.0, in1=r_near[:, :],
                                                   op0=ALU.subtract, op1=ALU.mult).then_inc(neg_out, 1)
                if has(1):
                    maxima(u + 1, 1, (0,))
                if has(-1):
                    dve.wait_ge(neg_out, u)
                    dve.wait_ge(o_done, u)
                    nc.vector.scalar_tensor_tensor(
                        out=of(attn_t, at(-1, 4), slice(b * S, (b + 1) * S)).rearrange("p o s -> p (o s)"),
                        in0=o_ps, scalar=-1.0, in1=r_neg[:, :], op0=ALU.mult, op1=ALU.mult).then_inc(o_out, 1)
                if has(1):
                    maxima(u + 1, 1, (1, 2))
                    dve.wait_ge(max_out, (u + 2) * 6)
                    nc.vector.tensor_scalar(shift[:, :, :, 0], row_max[:, :, :], -1.0, None,
                                            ALU.mult).then_inc(shift_hi_out, 1)
                    dve.wait_ge(shift_hi_out, u + 2)
                    nc.vector.scalar_tensor_tensor(out=shift[:, :, :, 1], in0=row_max[:, :, :], scalar=-1.0,
                                                   in1=shift[:, :, :, 0], op0=ALU.mult,
                                                   op1=ALU.subtract).then_inc(shift_out, 1)
                if has(2):
                    for w, h in ((1, 0), (0, 0), (0, 1), (1, 1)):
                        ready, hi, out, done = ((qh_out, q_hihi, q_lo, ql_out), (kh_out, k_hilo, k_hilo, kl_out))[w]
                        dve.wait_ge(ready, u * 2 + (5 + h))
                        nc.vector.scalar_tensor_tensor(
                            out=out[(SPLIT, OTHER)[w][h], par, h, :], in0=aux[w][SPLIT[h], :],
                            scalar=bias_qk[SPLIT[h], w, bass.ds(at(2, 4), 1)],
                            in1=hi[SPLIT[h], par, h, :].bitcast(f32), op0=ALU.add, op1=ALU.subtract,
                        ).then_inc(done, 1)

            for b in range(B):
                dve.wait_ge(x_hi_out, b + 1)
                xs = slice(b * S, (b + 1) * S)
                nc.vector.tensor_tensor(x_lo[:, xs], x_t[:, xs], x_hi[:, xs].bitcast(f32),
                                        ALU.subtract).then_inc(x_lo_out, 1)
            dve.wait_ge(const_in, CONSTS)
            dve.wait_ge(filled, 2)
            for u in (-2, -1, 0):
                slot(*known(u))
            with dve.Fori(0, LOOPS) as p:
                for k in range(1, 5):
                    slot(*looped(p, k))
            for u in PEELED:
                slot(*known(u))

        @block.gpsimd
        def _(pool):
            def split_w(pair):
                pool.wait_ge(k_done, least(pair * 4))
                pool.sem_inc(passed, 1)
                nc.gpsimd.tensor_copy(w_hi[:, :, :], of(w_all, pair, slice(0, 2), slice(None)).rearrange(
                    "p o w d -> p (o w) d")).then_inc(w_hi_out, 1)
                pool.wait_ge(w_hi_out, pair + 1)
                pool.sem_inc(passed, 1)
                nc.gpsimd.tensor_tensor(w_lo[:, :, :], of(w_all, pair, slice(0, 2), slice(None)).rearrange(
                    "p o w d -> p (o w) d"), w_hi[:, :, :].bitcast(f32), ALU.subtract).then_inc(w_lo_out, 1)

            def slot(u, m, has, at):
                par = m % 2
                if m == 2 and has(2):
                    split_w(at(2, 4))
                if has(0):
                    pool.wait_ge(r_done, least(u - 1))
                    pool.sem_inc(passed, 1)
                    p, acc = probs[:, par, :, :], p_sum[:, par, :, :]
                    for h in (0, 1):
                        pool.wait_ge(exp_out, u * 4 + (2 * h + 2))
                        pool.sem_inc(passed, 1)
                        for src, step in ((0, 512), (1152, 128)):
                            blk = p[:, h, src:src + 2 * step].rearrange("p (j c) -> p j c", j=2)[:, :, 0:T]
                            last = nc.gpsimd.affine_select(out=blk, in_=blk, compare_op=ALU.is_ge, fill=0.0, base=0,
                                                           pattern=[[0, 2], [1, T]], channel_multiplier=-1)
                        last.then_inc(masked, 1)
                        pool.wait_ge(masked, u * 2 + (h + 1))
                        if h == 0:
                            nc.gpsimd.tensor_tensor(acc[:, 0, :], p[:, 0, T:S], p[:, 0, 512:896], ALU.add).then_inc(added, 1)
                    for h in (0, 1):
                        if h == 1:
                            nc.gpsimd.tensor_tensor(acc[:, 1, :], p[:, 1, T:S], p[:, 1, 512:896], ALU.add).then_inc(added, 1)
                        pool.wait_ge(added, u * 4 + (2 * h + 1))
                        nc.gpsimd.tensor_tensor(acc[:, h, T:], acc[:, h, T:], p[:, h, 1280:1536], ALU.add).then_inc(added, 1)
                        pool.wait_ge(added, u * 4 + (2 * h + 2))
                        nc.gpsimd.tensor_tensor(acc[:, h, 2 * T:], acc[:, h, 2 * T:], p[:, h, 1152:1280],
                                                ALU.add).then_inc(summed, 1)

            nc.gpsimd.memset(ones64[:, :], 1.0)
            for t in (k_hi1, q_lo):
                nc.gpsimd.memset(t[:, :, :, :].bitcast(f32), 0.0)
            nc.gpsimd.drain()
            nc.gpsimd.memset(k_hi1[64:66, :, 0, :].bitcast(f32), 1.0).then_inc(filled, 1)
            nc.gpsimd.memset(k_hi1[0:2, :, 1, :].bitcast(f32), 1.0).then_inc(filled, 1)
            pool.wait_ge(filled, 2)
            pool.wait_ge(w_in, 16)
            for u in (-2, -1, 0):
                slot(*known(u))
                if u == -2:
                    pool.wait_ge(w_rest_in, 16)
            with pool.Fori(0, LOOPS) as p:
                for k in range(1, 5):
                    slot(*looped(p, k))
            for u in PEELED:
                slot(*known(u))

        @block.sync
        def _(sp):
            def slot(u, m, has, at):
                par = m % 2
                if has(2):
                    for h in (0, 1):
                        sp.wait_ge(qh_out, u * 2 + (5 + h))
                        sp.dma_start(q_hihi[OTHER[h], par, h, :].bitcast(f32),
                                     q_hihi[SPLIT[h], par, h, :].bitcast(f32)).then_inc(q_dup[par][h], 16)
                    for h in (0, 1):
                        sp.wait_ge(kh_out, u * 2 + (5 + h))
                        sp.dma_start(k_hi1[SPLIT[h], par, h, :].bitcast(f32),
                                     k_hilo[SPLIT[h], par, h, :].bitcast(f32)).then_inc(k_dup[par][h], 16)

            sp.dma_start(w_all[:, 0, :, :], w_qkv[:, 0, :, :]).then_inc(w_in, 16)
            for b in range(B):
                sp.dma_start(x_t[:, b * S:(b + 1) * S], xT[:, b * S:(b + 1) * S]).then_inc(x_in[b], 16)
                if b == 0:
                    sp.dma_start(bias_qk[:, :, :], b_qk).then_inc(const_in, 16)
                    sp.dma_start(neg_mask[:, :], causal).then_inc(const_in, 16)
                    sp.dma_start(ident_b[:, :], ident).then_inc(const_in, 16)
            sp.dma_start(w_all[:, 1:, :, :], w_qkv[:, 1:, :, :]).then_inc(w_rest_in, 16)
            for dst, src in later:
                sp.dma_start(dst, src).then_inc(later_in, 16)
            sp.wait_ge(filled, 2)
            for u in (-2, -1, 0):
                slot(*known(u))
            with sp.Fori(0, LOOPS) as p:
                for k in range(1, 5):
                    slot(*looped(p, k))
            for u in PEELED:
                slot(*known(u))


HX, DK = 16, 8
C = 77
F = 128
EPS = 1e-5


def rest_of_layer(nc, banks, attn_t, consts, consts_in, x_nat, out):
    wo_s, bo_s, bv_s, ctx_s, wx_s, hmask, gmask, id_f, id_b, fk_s, sc_s, fb_s = consts
    f32, bf16, i32 = mybir.dt.float32, mybir.dt.bfloat16, mybir.dt.int32
    ALU, ACT, AX = mybir.AluOpType, mybir.ActivationFunctionType, mybir.AxisListType
    ctx = ExitStack()
    with ctx:
        sb = lambda name, shape, dt=f32: ctx.enter_context(nc.sbuf_tensor(name, shape, dt))
        sem = lambda name: ctx.enter_context(nc.semaphore(name))
        two = lambda name, shape, dt=f32: [sb(f"{name}{j}", shape, dt) for j in range(2)]

        bias_y = sb("bias_y", [128, 1])
        fkq = sb("fkq", [128, F], bf16)
        sc_r = sb("sc_r", [128, 2])
        sc_p = sb("sc_p", [128, 1])
        gm_c = sb("gm_c", [C, 4, 32])
        halves = sb("halves", [128, NT])
        k2_s = sb("k2_s", [128, B, C])
        v2_s = sb("v2_s", [C, B, E])
        k_heads = two("k_heads", [128, HX, C])
        v_heads = two("v_heads", [C, 4, 4, 32])
        x_s = sb("x_s", [128, B, NT, E])
        y_out = sb("y_out", [128, B, NT, E])
        y_t = two("y_t", [128, S])
        r_s = two("r_s", [128, NT, E])
        stats = two("stats", [128, NT, 6])
        mv = two("mv", [128, NT, 2])
        var_e = two("var_e", [128, NT])
        rstd = two("rstd", [128, NT])
        xn = two("xn", [128, NT, E])
        q2_t = two("q2_t", [128, S])
        mx = two("mx", [128, HX])
        ex = two("ex", [128, HX, C])
        p_t = sb("p_t", [C, 2, HX, T])
        rs2 = two("rs2", [128, S])
        x_b = two("x_b", [128, S], bf16)
        qv = two("qv", [128, S])
        qm = two("qm", [128, S])
        xq = two("xq", [128, S], bf16)
        xq_t = two("xq_t", [128, S], bf16)
        y_b = two("y_b", [128, S], bf16)
        scores = banks[:, 4:8, 0:4 * C].rearrange("p b (h k) -> p b h k", h=4)
        own = [banks[:, 2, :], banks[:, 3, :]]
        wo_ps = [banks[:, 4, :], banks[:, 5, :]]
        tp = [banks[:, 0, :], banks[:, 1, :]]
        tpb = [banks[:, j, 0:S // 2].bitcast(bf16) for j in range(2)]
        PER = 2 * (3 + 1 + 3 + 1 + 8 + 4)
        TWO_PER_TILE, ACT_PARTS = 2 * 2 * NT, 3 * 2 * NT

        (x_nat_in, kv_done, kv_out, heads_out, wo_done, wo_out, y_done, var_out, rstd_out, norm_out, xt_done,
         xt_out, q2_done, q2_out, sc_done, sc_out, max2_out, exp2_out, pt_done, pt_act_out, pt_dve_out, pv_done, o2_out,
         y2_done, quant_out, xqt_done, xqt_out, y3_done, y3_out, link_done, passed2, ffn_k_out, halves_out) = (
            sem(n + "_x") for n in ("""x_nat_in kv_done kv_out heads_out wo_done wo_out y_done var_out rstd_out
            norm_out xt_done xt_out q2_done q2_out sc_done sc_out max2_out exp2_out pt_done pt_act_out pt_dve_out pv_done
            o2_out y2_done quant_out xqt_done xqt_out y3_done y3_out link_done passed2 ffn_k_out halves_out""").split())

        stored = sem("stored")
        LOADS = 16 * len(consts)
        block = ctx.enter_context(nc.Block())

        @block.sync
        def _(sp):
            sp.dma_start(x_s[:, :, :, :], x_nat).then_inc(x_nat_in, 16)
            with sp.Fori(0, B // 2) as it:
                for j in (0, 1):
                    n = it * 2 + j
                    sp.wait_ge(norm_out, it * 6 + (4 + j + 1))
                    sp.dma_start(out[n, :, :, :], y_out[:, bass.ds(n, 1), :, :].rearrange("p o i e -> p (o i) e")
                                 ).then_inc(stored, 16)
            sp.wait_ge(stored, 16 * B)

        @block.tensor
        def _(pe):
            mm = nc.tensor.matmul
            pe.wait_ge(consts_in, LOADS)
            mm(own[0][:, 0:B * C], wx_s[:, 1, :], ctx_s[:, :, :].rearrange("p b k -> p (b k)"),
               start=True, stop=True).then_inc(kv_done, 1)
            for b in range(B):
                last = mm(own[1][0:C, b * E:(b + 1) * E], ctx_s[:, b, :], wx_s[:, 2, :], start=True, stop=True)
            last.then_inc(kv_done, 1)
            for p in range(PAIRS):
                last = mm(tp[0][:, 0:1], wo_s[:, p, :], bv_s[:, p:p + 1], start=(p == 0), stop=(p == PAIRS - 1))
            last.then_inc(kv_done, 1)
            pe.wait_ge(kv_out, 2)

            def four(dst, lhs, rhs, done, transpose=False):
                for i in range(NT):
                    sl = slice(i * T, (i + 1) * T)
                    if transpose:
                        last = nc.tensor.transpose(dst[:, sl], lhs(i), rhs)
                    else:
                        last = mm(dst[:, sl], lhs(i), rhs, start=True, stop=True)
                last.then_inc(done, 1)

            J = (0, 1)

            def project(it):
                for j in J:
                    for p in range(PAIRS):
                        last = mm(wo_ps[j], wo_s[:, p, :], attn_t[:, p, (it * 2 + j) * S:(it * 2 + j + 1) * S],
                                  start=(p == 0), stop=(p == PAIRS - 1))
                    last.then_inc(wo_done, 1)

            def round(it):
                n = lambda j: it * 2 + (j + 1)
                for j in J:
                    pe.wait_ge(wo_out, n(j))
                    four(own[j], lambda i: y_t[j][:, i * T:(i + 1) * T], id_f[:, :], y_done, True)
                for j in J:
                    pe.wait_ge(norm_out, it * 6 + (j + 1))
                    four(own[j], lambda i: xn[j][:, i, :], id_f[:, :], xt_done, True)
                for j in J:
                    pe.wait_ge(xt_out, n(j))
                    mm(own[j], wx_s[:, 0, :], r_s[j][:, :, :].rearrange("p i e -> p (i e)"),
                       start=True, stop=True).then_inc(q2_done, 1)
                pe.wait_ge(q2_out, n(1))
                pe.wait_ge(heads_out, n(1))

                def score(t):
                    j, i = divmod(t, NT)
                    for g in (0, 1):
                        if t > 0:
                            pe.wait_ge(sc_out, it * TWO_PER_TILE + (2 * t + g - 1))
                        for c in (2 * g, 2 * g + 1):
                            last = mm(banks[:, 4 + c, 0:4 * C], q2_t[j][:, i * T:(i + 1) * T],
                                      k_heads[j][:, 4 * c:4 * c + 4, :].rearrange("p h k -> p (h k)"),
                                      start=True, stop=True)
                        last.then_inc(sc_done, 1)

                def transposes(t, f):
                    for h in range(4):
                        last = nc.tensor.transpose(tp[f % 2][0:C, h * T:(h + 1) * T], ex[t % 2][:, 4 * f + h, :],
                                                   id_f[:, :])
                    last.then_inc(pt_done, 1)

                def weigh(t, part):
                    j, i = divmod(t, NT)
                    for a in range(4):
                        for g in range(4):
                            last = mm(own[part][32 * g:32 * g + 32, i * T:(i + 1) * T],
                                      (gm_c[:, a, :], v_heads[j][:, g, a, :])[part], p_t[:, t % 2, 4 * g + a, :],
                                      start=(a == 0), stop=(a == 3))
                    return last

                score(0)
                for t in range(2 * NT + 1):
                    if t + 1 < 2 * NT:
                        score(t + 1)
                    for part in (0, 1):
                        if t < 2 * NT:
                            if part == 0:
                                pe.wait_ge(exp2_out, it * (2 * NT) + (t + 1))
                            if part == 1 or t > 0:
                                pe.wait_ge(pt_act_out, it * ACT_PARTS + (3 * t - 1 + 2 * part))
                            transposes(t, 2 * part)
                            if part == 1:
                                pe.wait_ge(pt_dve_out, it * (2 * NT) + (t + 1))
                            elif t > 0:
                                pe.wait_ge(pt_act_out, it * ACT_PARTS + 3 * t)
                            transposes(t, 2 * part + 1)
                        if t > 0:
                            if part == 0:
                                pe.wait_ge(pt_act_out, it * ACT_PARTS + 3 * t)
                                pe.wait_ge(pt_dve_out, it * (2 * NT) + t)
                                if t == NT + 1:
                                    pe.wait_ge(o2_out, n(0))
                            last = weigh(t - 1, part)
                            if part == 1:
                                last.then_inc(pv_done, 1)
                for j in J:
                    pe.wait_ge(o2_out, n(1))
                    four(own[j], lambda i: y_t[j][:, i * T:(i + 1) * T], wx_s[:, 3, :], y2_done)
                if it + 1 < B // 2:
                    pe.wait_ge(sc_out, (it + 1) * TWO_PER_TILE)
                    project(it + 1)
                for j in J:
                    pe.wait_ge(quant_out, n(j))
                    four(tpb[j], lambda i: xq[j][:, i * T:(i + 1) * T], id_b[:, :], xqt_done, True)
                for j in J:
                    pe.wait_ge(xqt_out, n(j))
                    pe.wait_ge(ffn_k_out, 1)
                    four(own[j], lambda i: xq_t[j][:, i * T:(i + 1) * T], fkq[:, :], y3_done)
                pe.wait_ge(y3_out, n(1))

            project(0)
            for it in range(B // 2):
                round(it)

        @block.scalar
        def _(act):
            copy = nc.scalar.copy
            act.wait_ge(kv_done, 1)
            copy(k2_s[:, :, :].rearrange("p b k -> p (b k)"), own[0][:, 0:B * C]).then_inc(kv_out, 1)
            act.wait_ge(kv_done, 2)
            copy(v2_s[:, :, :].rearrange("p b e -> p (b e)"), own[1][0:C, :]).then_inc(kv_out, 1)
            act.wait_ge(consts_in, LOADS)
            act.wait_ge(kv_done, 3)
            nc.scalar.activation(bias_y[:, :], tp[0][:, 0:1], ACT.Identity, bias=bo_s[:, 0:1]).then_inc(kv_out, 1)
            act.wait_ge(kv_out, 3)
            with act.Fori(0, B // 2) as it:
                J = (0, 1)
                n = lambda j: it * 2 + (j + 1)
                for j in J:
                    act.wait_ge(wo_done, n(j))
                    nc.scalar.activation(y_t[j][:, :], wo_ps[j], ACT.Identity, bias=bias_y[:, 0:1]).then_inc(wo_out, 1)
                for j in J:
                    act.wait_ge(xt_done, n(j))
                    copy(r_s[j][:, :, :].rearrange("p i e -> p (i e)"), own[j]).then_inc(xt_out, 1)
                for j in J:
                    act.wait_ge(q2_done, n(j))
                    copy(q2_t[j][:, :], own[j]).then_inc(q2_out, 1)
                for t in range(2 * NT):
                    act.wait_ge(sc_out, it * TWO_PER_TILE + (2 * t + 2))
                    nc.scalar.activation(ex[t % 2][:, :, :], ex[t % 2][:, :, :], ACT.Exp,
                                         scale=DK ** -0.5).then_inc(exp2_out, 1)
                    for f in (0, 2, 3):
                        act.wait_ge(pt_done, it * (8 * NT) + (4 * t + f + 1))
                        copy(p_t[:, t % 2, 4 * f:4 * f + 4, :],
                             tp[f % 2][0:C, :].rearrange("p (h s) -> p h s", h=4)).then_inc(pt_act_out, 1)
                for j in J:
                    act.wait_ge(xqt_done, n(j))
                    copy(xq_t[j][:, :], tpb[j]).then_inc(xqt_out, 1)
                for j in J:
                    act.wait_ge(y3_done, n(j))
                    act.wait_ge(ffn_k_out, 1)
                    nc.scalar.activation(y_b[j][:, :], own[j], ACT.Copy, scale=sc_p[:, 0:1]).then_inc(y3_out, 1)

        @block.gpsimd
        def _(pool):
            nc.gpsimd.memset(halves[:, :], -0.5).then_inc(halves_out, 1)
            pool.wait_ge(halves_out, 1)
            with pool.Fori(0, B // 2) as it:
                for l in range(3):
                    for j in (0, 1):
                        c = it * 6 + (2 * l + j + 1)
                        pool.wait_ge(var_out, c)
                        nc.gpsimd.tensor_tensor(rstd[j][:, :], var_e[j][:, :], halves[:, :], ALU.pow).then_inc(rstd_out, 1)

        @block.vector
        def _(dve):
            V = nc.vector
            made = [0, None]

            def link(ins):
                made[0] += 1
                ins.then_inc(link_done, 1)
                dve.wait_ge(link_done, made[0] if made[1] is None else made[1] + made[0])
                dve.sem_inc(passed2, 1)

            def chain(steps, batches=(0, 1)):
                before = [None] * 2
                for step in steps:
                    for j in batches:
                        if before[j] is not None:
                            dve.wait_ge(link_done, before[j] if made[1] is None else made[1] + before[j])
                            dve.sem_inc(passed2, 1)
                        step(j).then_inc(link_done, 1)
                        made[0] += 1
                        before[j] = made[0]

            def rounding(src, scale_r, v, m):
                return (
                    lambda j: V.tensor_scalar(v(j), src(j), scale_r, None, ALU.mult),
                    lambda j: V.tensor_single_scalar(m(j).bitcast(i32), v(j).bitcast(i32), 0x7F800000, ALU.bitwise_and),
                    lambda j: V.tensor_scalar(m(j), m(j), 2.0 ** -6, 1.5 * 2 ** 20, ALU.max, ALU.mult),
                    lambda j: V.tensor_tensor(v(j), v(j), m(j), ALU.add),
                    lambda j: V.tensor_tensor(v(j), v(j), m(j), ALU.subtract),
                    lambda j: V.tensor_tensor(m(j), v(j), v(j), ALU.mult),
                    lambda j: V.tensor_scalar(m(j), m(j), 448.0 ** 2, 3.0e38, ALU.is_gt, ALU.mult),
                    lambda j: V.tensor_scalar(m(j), m(j), 3.0e38, 0.0, ALU.mult, ALU.mult))

            def bn(j):
                for i in range(NT):
                    last = V.bn_stats(out=stats[j][:, i, :], in_=r_s[j][:, i, :])
                return last

            def aggregate(j):
                for i in range(NT):
                    last = V.bn_aggr(out=mv[j][:, i, :], in_=stats[j][:, i, :])
                return last

            def layernorm(*residual):
                chain(residual + (bn, aggregate))
                for j in (0, 1):
                    dve.wait_ge(link_done, made[1] + made[0] - 1 + j)
                    dve.sem_inc(passed2, 1)
                    V.tensor_scalar(var_e[j][:, :], mv[j][:, :, 1], EPS, None, ALU.add).then_inc(var_out, 1)

            dve.wait_ge(consts_in, LOADS)
            V.tensor_copy(gm_c[:, :, :], gmask[0:C, :, :])
            link(V.reciprocal(sc_r[:, :], sc_s[:, :]))
            link(V.tensor_tensor(sc_p[:, :], sc_s[:, 0:1], sc_s[:, 1:2], ALU.mult))
            chain(rounding(lambda j: fk_s[:, :], sc_r[:, 1:2], lambda j: qv[0][:, 0:F], lambda j: qm[0][:, 0:F]), (0,))
            dve.wait_ge(link_done, made[0])
            V.tensor_tensor(fkq[:, :], qv[0][:, 0:F], qm[0][:, 0:F], ALU.add).then_inc(ffn_k_out, 1)
            dve.wait_ge(kv_out, 2)
            dve.wait_ge(x_nat_in, 16)
            base = made[0]
            with dve.Fori(0, B // 2) as it:
                made[0] = base
                made[1] = it * PER
                J = (0, 1)
                n = lambda j: it * 2 + (j + 1)
                flat = lambda t: t[:, :, :].rearrange("p i e -> p (i e)")
                for j in J:
                    b = it * 2 + j
                    V.tensor_tensor(k_heads[j][:, :, :], k2_s[:, bass.ds(b, 1), :].broadcast_to([128, HX, C]),
                                    hmask[:, :].unsqueeze(2).broadcast_to([128, HX, C]), ALU.mult)
                    for g in range(4):
                        last = V.tensor_tensor(
                            v_heads[j][:, g, :, :],
                            v2_s[:, bass.ds(b, 1), 32 * g:32 * g + 32].broadcast_to([C, 4, 32]),
                            gmask[0:C, :, :], ALU.mult)
                    last.then_inc(heads_out, 1)
                def add_heads(j):
                    dve.wait_ge(y_done, n(j))
                    return V.tensor_tensor(flat(r_s[j]), own[j],
                                           x_s[:, bass.ds(it * 2 + j, 1), :, :].rearrange("p o i e -> p (o i e)"), ALU.add)

                layernorm(add_heads)
                for j in J:
                    dve.wait_ge(rstd_out, it * 6 + (j + 1))
                    for i in range(NT):
                        last = V.tensor_scalar(xn[j][:, i, :], r_s[j][:, i, :], mv[j][:, i, 0:1], rstd[j][:, i:i + 1],
                                               ALU.subtract, ALU.mult)
                    last.then_inc(norm_out, 1)
                half = lambda m, g: m[:, 8 * g:8 * g + 8].rearrange("p (b h) -> p b h", b=2)

                def evacuate(t):
                    dve.wait_ge(pt_done, it * (8 * NT) + (4 * t + 2))
                    V.tensor_copy(p_t[:, t % 2, 4:8, :],
                                  tp[1][0:C, :].rearrange("p (h s) -> p h s", h=4)).then_inc(pt_dve_out, 1)

                def normalise(j):
                    dve.wait_ge(pv_done, it * (2 * NT) + NT * (j + 1))
                    link(V.reciprocal(rs2[j][:, :], own[0]))
                    V.tensor_tensor(y_t[j][:, :], own[1], rs2[j][:, :], ALU.mult).then_inc(o2_out, 1)

                for t in range(2 * NT):
                    for g in (0, 1):
                        dve.wait_ge(sc_done, it * TWO_PER_TILE + (2 * t + g + 1))
                        V.tensor_reduce(half(mx[t % 2], g), scores[:, 2 * g:2 * g + 2, :, :],
                                        axis=AX.X, op=ALU.max).then_inc(max2_out, 1)
                    if t > 0:
                        evacuate(t - 1)
                    for g in (0, 1):
                        dve.wait_ge(max2_out, it * TWO_PER_TILE + (2 * t + g + 1))
                        dve.sem_inc(passed2, 1)
                        if t > 1:
                            dve.wait_ge(pt_done, it * (8 * NT) + (4 * t - 4))
                        V.tensor_tensor(ex[t % 2][:, 8 * g:8 * g + 8, :].rearrange("p (b h) k -> p b h k", b=2),
                                        scores[:, 2 * g:2 * g + 2, :, :],
                                        half(mx[t % 2], g).unsqueeze(3).broadcast_to([128, 2, 4, C]),
                                        ALU.subtract).then_inc(sc_out, 1)
                    if t == NT + 1:
                        normalise(0)
                evacuate(2 * NT - 1)
                normalise(1)
                def add_context(j):
                    dve.wait_ge(y2_done, n(j))
                    return V.tensor_tensor(flat(r_s[j]), own[j], flat(xn[j]), ALU.add)

                def add_bias(j):
                    dve.wait_ge(y3_out, n(j))
                    return V.tensor_tensor(xq[j][:, :].rearrange("p (i e) -> p i e", i=NT),
                                           y_b[j][:, :].rearrange("p (i e) -> p i e", i=NT),
                                           fb_s[:, :].unsqueeze(1).broadcast_to([128, NT, F]), ALU.add)

                def add_ffn(j):
                    return V.tensor_tensor(flat(r_s[j]), xq[j][:, :], flat(xn[j]), ALU.add)

                for l in (1, 2):
                    if l == 2:
                        chain((lambda j: V.tensor_copy(x_b[j][:, :], flat(xn[j])),)
                              + rounding(lambda j: x_b[j][:, :], sc_r[:, 0:1], lambda j: qv[j][:, :], lambda j: qm[j][:, :]))
                        for j in J:
                            dve.wait_ge(link_done, made[1] + made[0] - 1 + j)
                            dve.sem_inc(passed2, 1)
                            V.tensor_tensor(xq[j][:, :], qv[j][:, :], qm[j][:, :], ALU.add).then_inc(quant_out, 1)
                        layernorm(add_bias, add_ffn)
                    else:
                        layernorm(add_context)
                    for j in J:
                        dve.wait_ge(rstd_out, it * 6 + (2 * l + j + 1))
                        for i in range(NT):
                            dst = xn[j][:, i, :] if l == 1 else y_out[:, bass.ds(it * 2 + j, 1), i, :].rearrange("p o e -> p (o e)")
                            last = V.tensor_scalar(dst, r_s[j][:, i, :], mv[j][:, i, 0:1],
                                                   rstd[j][:, i:i + 1], ALU.subtract, ALU.mult)
                        last.then_inc(norm_out, 1)
                        dve.wait_ge(norm_out, it * 6 + (2 * l + j + 1))
                assert made[0] - base == PER, made[0] - base


_INS = ["xT", "w_qkv", "b_qk", "b_v", "causal", "ident", "x_nat", "wo", "b_o", "ctx_t", "w_x", "head_mask",
        "group_mask", "ident_f", "ffn_k", "scales", "ffn_b"]


def program(nc, a, out):
    ctx = ExitStack()
    with ctx:
        banks = ctx.enter_context(nc.psum_tensor("banks", [128, 8, 512], mybir.dt.float32))
        attn_t = ctx.enter_context(nc.sbuf_tensor("attn_t", [128, PAIRS, B * S], mybir.dt.float32))
        f32, bf16 = mybir.dt.float32, mybir.dt.bfloat16
        consts, later = [], []
        for name, shape, dt in (("wo", [128, PAIRS, E], f32), ("b_o", [128, 1], f32), ("b_v", [128, PAIRS], f32),
                                ("ctx_t", [128, B, C], f32), ("w_x", [128, 4, E], f32), ("head_mask", [128, HX], f32),
                                ("group_mask", [128, 4, 32], f32), ("ident_f", [128, 128], f32),
                                ("ident", [128, 128], bf16), ("ffn_k", [128, F], bf16), ("scales", [128, 2], f32),
                                ("ffn_b", [128, F], bf16)):
            t = ctx.enter_context(nc.sbuf_tensor(name + "_s", shape, dt))
            consts.append(t)
            later.append((t[tuple(slice(None) for _ in shape)], a[name]))
        consts_in = ctx.enter_context(nc.semaphore("consts_in"))
        self_attention(nc, banks, attn_t, a["xT"], a["w_qkv"], a["b_qk"], a["causal"], a["ident"], later, consts_in)
        rest_of_layer(nc, banks, attn_t, consts, consts_in, a["x_nat"], out)


def kernel(**inputs):
    import concourse.bacc as bacc
    from concourse.bass_utils import run_bass_kernel_spmd as run

    g = {k: np.asarray(v) for k, v in inputs.items()}
    pairs = lambda w: w.transpose(1, 0, 2).reshape(E, PAIRS, 2 * D).transpose(1, 0, 2)
    x = g["x"]
    bf = g["L0_ffn_kernel"].dtype
    mask = np.zeros((T, S), np.float32)
    mask[:, S - T:] = np.where(np.arange(T)[None] > np.arange(T)[:, None], -3.0e38, 0.0)
    lay = {
        "xT": x.reshape(B * S, E).T,
        "w_qkv": np.stack([pairs(g["L0_attn_W" + n]) for n in "qkv"], 2).transpose(1, 0, 2, 3),
        "b_qk": np.stack([g["L0_attn_b" + n].reshape(PAIRS, 2 * D).T for n in "qk"], 1),
        "b_v": g["L0_attn_bv"].reshape(PAIRS, 2 * D).T,
        "causal": mask,
        "ident": np.eye(128).astype(bf),
        "x_nat": x.reshape(B, NT, T, E).transpose(2, 0, 1, 3),
        "wo": g["L0_attn_Wo"].reshape(PAIRS, 2 * D, E).transpose(1, 0, 2),
        "b_o": g["L0_attn_bo"].reshape(E, 1),
        "ctx_t": g["ctx_1024"].transpose(2, 0, 1),
        "w_x": np.stack([g["L0_xattn_W" + n].T for n in "qkvo"], 1),
        "head_mask": np.repeat(np.eye(HX, dtype=np.float32), DK, 0),
        "group_mask": np.broadcast_to(np.repeat(np.eye(4, dtype=np.float32), DK, 1), (128, 4, 32)),
        "ident_f": np.eye(128, dtype=np.float32),
        "ffn_k": g["L0_ffn_kernel"],
        "scales": np.broadcast_to(np.stack([g["L0_ffn_input_scale"], g["L0_ffn_kernel_scale"]], 1), (128, 2)),
        "ffn_b": np.broadcast_to(g["L0_ffn_bias"], (128, F)),
    }
    lay = {k: np.ascontiguousarray(v) for k, v in lay.items()}
    nc = bacc.Bacc("TRN2", target_bir_lowering=False, num_devices=1)
    a = {k: nc.dram_tensor(k, lay[k].shape, mybir.dt.from_np(lay[k].dtype), kind="ExternalInput").ap() for k in _INS}
    out = nc.dram_tensor("out", (B, T, NT, E), mybir.dt.float32, kind="ExternalOutput").ap()
    program(nc, a, out)
    r = run(nc, [lay], core_ids=[0])
    return r.results[0]["out"].transpose(0, 2, 1, 3).reshape(B, S, E)
```
